# Optimizing a Trainium2 kernel written in Bass

```python
import numpy as np
import jax
import jax.numpy as jnp

def _softmax(x, axis=-1):
    return jax.nn.softmax(x, axis=axis)

def _gelu(x):
    return jax.nn.gelu(x, approximate=True)

def _silu(x):
    return jax.nn.silu(x)

def _sigmoid(x):
    return jax.nn.sigmoid(x)

def _layernorm(x, axis=-1, eps=1e-05):
    m = jnp.mean(x, axis=axis, keepdims=True)
    v = jnp.var(x, axis=axis, keepdims=True)
    return (x - m) / jnp.sqrt(v + eps)

def _scatter_add(tgt, idx, src, axis=0):
    return tgt.at[idx].add(src)

def _segment_sum(src, seg, n):
    return jax.ops.segment_sum(src, seg, n)
kernel_name = 'mk_adaln_ffn_d4_seqx_r8_b9c47e'

def setup_inputs(seed: int=0):
    np.random.seed(seed)
    _w = jnp.asarray

    def _rec_inputs():
        import jax
        import jax.numpy as jnp
        _rk = jax.random.key(seed)
        x = 7.22e-05 + 1 * jax.random.normal(jax.random.fold_in(_rk, 1), (128, 32, 512), jnp.float32)
        _lenS = 32 - jax.random.randint(jax.random.fold_in(_rk, 7), (128,), 0, max(1, 32 // 4) + 1, jnp.int32)
        _lenS2 = 32 - jax.random.randint(jax.random.fold_in(_rk, 8), (128,), 0, max(1, 32 // 4) + 1, jnp.int32)
        itok_B_2_6 = jax.random.randint(jax.random.fold_in(_rk, 11), (128,), 2, 7, jnp.int32)
        itok_B_0_7 = jax.random.randint(jax.random.fold_in(_rk, 12), (128,), 0, 8, jnp.int32)
        itok_B_2182_4065 = jax.random.randint(jax.random.fold_in(_rk, 14), (128,), 2182, 4066, jnp.int32)
        itok_B_0_15 = jax.random.randint(jax.random.fold_in(_rk, 15), (128,), 0, 16, jnp.int32)
        itok_B_3_7 = jax.random.randint(jax.random.fold_in(_rk, 16), (128,), 3, 8, jnp.int32)
        return (x, itok_B_2_6, itok_B_0_7, itok_B_2182_4065, itok_B_0_15, itok_B_3_7, _lenS)
    x, itok_B_2_6, itok_B_0_7, itok_B_2182_4065, itok_B_0_15, itok_B_3_7, _lenS = _rec_inputs()

    def _L0_cond_setup():
        import jax, jax.numpy as jnp
        import numpy as np
        B, N, H, F = (4, 64, 512, 1376)
        L, R, RANK = (1, 16, 16)
        SCALE = 0.5
        key = jax.random.key(seed)
        ks = jax.random.split(key, 12)
        nrm = lambda k, shape, fan: jax.random.normal(k, shape, jnp.float32) * fan ** (-0.5)
        inp = {'x': jax.random.normal(ks[0], (B, N, H), jnp.float32), 'W_gate': nrm(ks[1], (F, H), H), 'W_up': nrm(ks[2], (F, H), H), 'W_down': nrm(ks[3], (H, F), F), 'A_gate': nrm(ks[4], (L, R, RANK, H), H), 'B_gate': nrm(ks[5], (L, R, F, RANK), RANK), 'A_up': nrm(ks[6], (L, R, RANK, H), H), 'B_up': nrm(ks[7], (L, R, F, RANK), RANK), 'A_down': nrm(ks[8], (L, R, RANK, F), F), 'B_down': nrm(ks[9], (L, R, H, RANK), RANK), 'lora_indices': jax.random.randint(ks[10], (B,), 0, R), 'layer_idx': 0}
        return inp
    _L0_cond_all = _L0_cond_setup()
    _L0_cond_in = {k: v for k, v in _L0_cond_all.items() if k in ('W_gate', 'W_up', 'W_down', 'A_gate', 'B_gate', 'A_up', 'B_up', 'A_down', 'B_down')}
    del _L0_cond_all

    def _L0_ffn_setup():
        import jax, jax.numpy as jnp
        import numpy as np
        HIDDEN = 512
        INTER = 1376
        GROUPSIZE = 128
        PACK = 8

        def dequant_gptq(qweight, scales, zeros, groupsize):
            K = qweight.shape[0] * PACK
            N = qweight.shape[1]
            k = jnp.arange(K)
            q = qweight[k // PACK, :] >> (k % PACK * 4)[:, None] & 15
            n = jnp.arange(N)
            z = zeros[:, n // PACK] >> (n % PACK * 4)[None, :] & 15
            s = scales.astype(jnp.float32)
            zp = (z.astype(jnp.float32) + 1.0) * s
            g = k // groupsize
            return q.astype(jnp.float32) * s[g] - zp[g]
        key = jax.random.key(seed)
        ks = jax.random.split(key, 11)
        imax = 2147483647
        G_h = HIDDEN // GROUPSIZE
        G_i = (INTER + GROUPSIZE - 1) // GROUPSIZE
        x = (jax.random.normal(ks[0], (2, 256, HIDDEN), dtype=jnp.float32) * 0.5).astype(jnp.float16)
        return {'x': x, 'gate_qweight': jax.random.randint(ks[1], (HIDDEN // PACK, INTER), 0, imax, dtype=jnp.int32), 'gate_scales': (jax.random.uniform(ks[2], (G_h, INTER), dtype=jnp.float32) * 0.01 + 0.001).astype(jnp.float16), 'gate_zeros': jax.random.randint(ks[3], (G_h, INTER // PACK), 0, imax, dtype=jnp.int32), 'up_qweight': jax.random.randint(ks[4], (HIDDEN // PACK, INTER), 0, imax, dtype=jnp.int32), 'up_scales': (jax.random.uniform(ks[5], (G_h, INTER), dtype=jnp.float32) * 0.01 + 0.001).astype(jnp.float16), 'up_zeros': jax.random.randint(ks[6], (G_h, INTER // PACK), 0, imax, dtype=jnp.int32), 'down_qweight': jax.random.randint(ks[7], (INTER // PACK, HIDDEN), 0, imax, dtype=jnp.int32), 'down_scales': (jax.random.uniform(ks[8], (G_i, HIDDEN), dtype=jnp.float32) * 0.01 + 0.001).astype(jnp.float16), 'down_zeros': jax.random.randint(ks[9], (G_i, HIDDEN // PACK), 0, imax, dtype=jnp.int32)}
    _L0_ffn_all = _L0_ffn_setup()
    _L0_ffn_in = {k: v for k, v in _L0_ffn_all.items() if k in ('gate_qweight', 'gate_scales', 'gate_zeros', 'up_qweight', 'up_scales', 'up_zeros', 'down_qweight', 'down_scales', 'down_zeros')}
    del _L0_ffn_all

    def _L1_cond_setup():
        import jax, jax.numpy as jnp
        import numpy as np
        SESSION_CHANNELS = [128, 160, 192, 224, 240, 248, 252, 32]
        N_SESS = len(SESSION_CHANNELS)
        B, MAX_C, MAX_T = (16, 32, 512)
        HID, N_SRC = (64, 32)
        key = jax.random.key(seed)
        ks = jax.random.split(key, 7)
        session_ids = jax.random.randint(ks[0], (B,), 0, N_SESS)
        chan_table = jnp.asarray(SESSION_CHANNELS)
        channel_counts = chan_table[session_ids]
        seq_lens = jax.random.randint(ks[1], (B,), MAX_T // 2, MAX_T + 1)
        x = jax.random.normal(ks[2], (B, MAX_C, MAX_T), jnp.float32)
        cmask = (jnp.arange(MAX_C)[None, :] < channel_counts[:, None]).astype(x.dtype)
        tmask = (jnp.arange(MAX_T)[None, :] < seq_lens[:, None]).astype(x.dtype)
        x = x * cmask[:, :, None] * tmask[:, None, :]
        lim1 = 1.0 / np.sqrt(MAX_C)
        W_sess = jax.random.uniform(ks[3], (N_SESS, MAX_C, HID), jnp.float32, -lim1, lim1)
        b_sess = jax.random.uniform(ks[4], (N_SESS, HID), jnp.float32, -lim1, lim1)
        lim2 = 1.0 / np.sqrt(HID)
        W2 = jax.random.uniform(ks[5], (HID, N_SRC), jnp.float32, -lim2, lim2)
        b2 = jax.random.uniform(ks[6], (N_SRC,), jnp.float32, -lim2, lim2)
        return dict(x=x, session_ids=session_ids, channel_counts=channel_counts, seq_lens=seq_lens, W_sess=W_sess, b_sess=b_sess, W2=W2, b2=b2)
    _L1_cond_all = _L1_cond_setup()
    _L1_cond_in = {k: v for k, v in _L1_cond_all.items() if k in ('W_sess', 'b_sess', 'W2', 'b2')}
    del _L1_cond_all

    def _L1_ffn_setup():
        import jax, jax.numpy as jnp
        import numpy as np
        NUM_EXPERTS = 8
        TOP_K = 2
        RANK = 16
        LORA_ALPHA = 32
        SCALING = LORA_ALPHA / RANK
        key = jax.random.key(seed)
        ks = jax.random.split(key, 6)
        B, S, D_IN, D_OUT = (4, 256, 512, 512)
        x = jax.random.normal(ks[0], (B, S, D_IN), dtype=jnp.float32)
        W_base = jax.random.normal(ks[1], (D_OUT, D_IN), dtype=jnp.float32) * 0.02
        b_base = jax.random.normal(ks[2], (D_OUT,), dtype=jnp.float32) * 0.02
        W_router = jax.random.normal(ks[3], (NUM_EXPERTS, D_IN), dtype=jnp.float32) * 0.02
        A = jax.random.normal(ks[4], (NUM_EXPERTS, RANK, D_IN), dtype=jnp.float32) * 0.02
        Bm = jax.random.normal(ks[5], (D_OUT, RANK), dtype=jnp.float32) * 0.02
        Bm = jnp.broadcast_to(Bm, (NUM_EXPERTS, D_OUT, RANK)) * jnp.arange(1, NUM_EXPERTS + 1, dtype=jnp.float32)[:, None, None] * 0.2
        return {'x': x, 'W_base': W_base, 'b_base': b_base, 'W_router': W_router, 'A': A, 'B': Bm}
    _L1_ffn_all = _L1_ffn_setup()
    _L1_ffn_in = {k: v for k, v in _L1_ffn_all.items() if k in ('W_base', 'b_base', 'W_router', 'A', 'B')}
    del _L1_ffn_all

    def _L2_cond_setup():
        import jax, jax.numpy as jnp
        import numpy as np
        NUM_CONDITIONS = 16
        IN_CH = 32
        OUT_CH = 32
        B = 64
        T = 512
        key = jax.random.key(seed)
        k_x, k_w, k_c = jax.random.split(key, 3)
        x = jax.random.normal(k_x, (B, IN_CH, T), dtype=jnp.float32)
        bound = float(np.sqrt(6.0 / IN_CH))
        weights = jax.random.uniform(k_w, (NUM_CONDITIONS, IN_CH, OUT_CH), dtype=jnp.float32, minval=-bound, maxval=bound)
        condition = jax.random.randint(k_c, (B,), 0, NUM_CONDITIONS, dtype=jnp.int64)
        return {'x': x, 'weights': weights, 'condition': condition}
    _L2_cond_all = _L2_cond_setup()
    _L2_cond_in = {k: v for k, v in _L2_cond_all.items() if k in ('weights',)}
    del _L2_cond_all

    def _L2_ffn_setup():
        import jax, jax.numpy as jnp
        import numpy as np

        def _block_dequantize_mixed(packed, scale, mask):
            q_lo = packed & 15
            q_hi = packed >> 4 & 15
            q = jnp.stack([q_lo, q_hi], axis=-1).reshape(packed.shape[0], -1)
            scale_eff = scale.astype(jnp.float32) * jnp.where(mask[:, None], 1.0, 0.5)
            return (q.astype(jnp.float32) - 8.0) * scale_eff
        key = jax.random.key(seed)
        k1, k2, k3, k4, k5 = jax.random.split(key, 5)
        B, S, IN, OUT, G = (8, 256, 512, 512, 32)
        NB = OUT * IN // G
        x = jax.random.normal(k1, (B, S, IN), dtype=jnp.float32)
        weight_packed = jax.random.randint(k2, (NB, G // 2), 0, 32, dtype=jnp.int32)
        weight_scale = (jax.random.uniform(k3, (NB, 1)) * 0.02).astype(jnp.float16)
        weight_var_mask = jax.random.randint(k4, (NB,), 0, 2) > 0
        bias = jax.random.normal(k5, (OUT,), dtype=jnp.float32)
        return {'x': x, 'weight_packed': weight_packed, 'weight_scale': weight_scale, 'weight_var_mask': weight_var_mask, 'bias': bias}
    _L2_ffn_all = _L2_ffn_setup()
    _L2_ffn_in = {k: v for k, v in _L2_ffn_all.items() if k in ('weight_packed', 'weight_scale', 'weight_var_mask', 'bias')}
    del _L2_ffn_all

    def _L3_cond_setup():
        import jax, jax.numpy as jnp
        import numpy as np
        MAX_LORAS, OUT, IN = (8, 512, 512)
        B, S = (4, 256)
        key = jax.random.key(seed)
        k1, k2, k3 = jax.random.split(key, 3)
        x = jax.random.normal(k1, (B, S, IN), dtype=jnp.float32)
        weight = jax.random.normal(k2, (MAX_LORAS, OUT, IN), dtype=jnp.float32) * 0.02
        adapter_ids = jax.random.randint(k3, (B,), 0, MAX_LORAS, dtype=jnp.int32)
        return {'x': x, 'weight': weight, 'adapter_ids': adapter_ids}
    _L3_cond_all = _L3_cond_setup()
    _L3_cond_in = {k: v for k, v in _L3_cond_all.items() if k in ('weight',)}
    del _L3_cond_all

    def _L3_ffn_setup():
        import jax, jax.numpy as jnp
        import numpy as np
        RANKS = (8, 16, 32, 64)
        TOPK = 1
        SCALING = 1.0 / 4
        key = jax.random.key(seed)
        ks = jax.random.split(key, 7)
        D_IN, D_OUT, MAX_R, N_RANKS = (512, 512, 64, len(RANKS))
        B_, S_ = (4, 256)
        return {'hidden_states': jax.random.normal(ks[0], (B_, S_, D_IN), jnp.float32), 'W': jax.random.normal(ks[1], (D_OUT, D_IN), jnp.float32) * 0.02, 'b': jax.random.normal(ks[2], (D_OUT,), jnp.float32) * 0.02, 'A': jax.random.normal(ks[3], (MAX_R, D_IN), jnp.float32) * 0.02, 'B': jnp.zeros((D_OUT, MAX_R), jnp.float32) + jax.random.normal(ks[4], (D_OUT, MAX_R), jnp.float32) * 0.02, 'gate_w': jax.random.normal(ks[5], (N_RANKS, D_IN), jnp.float32) * 0.02, 'gate_b': jax.random.normal(ks[6], (N_RANKS,), jnp.float32) * 0.02}
    _L3_ffn_all = _L3_ffn_setup()
    _L3_ffn_in = {k: v for k, v in _L3_ffn_all.items() if k in ('W', 'b', 'A', 'B', 'gate_w', 'gate_b')}
    del _L3_ffn_all
    return {'x': x, 'itok_B_2_6': itok_B_2_6, 'itok_B_0_7': itok_B_0_7, 'itok_B_2182_4065': itok_B_2182_4065, 'itok_B_0_15': itok_B_0_15, 'itok_B_3_7': itok_B_3_7, '_lenS': _lenS, 'L0_cond_W_gate': _L0_cond_in['W_gate'], 'L0_cond_W_up': _L0_cond_in['W_up'], 'L0_cond_W_down': _L0_cond_in['W_down'], 'L0_cond_A_gate': _L0_cond_in['A_gate'], 'L0_cond_B_gate': _L0_cond_in['B_gate'], 'L0_cond_A_up': _L0_cond_in['A_up'], 'L0_cond_B_up': _L0_cond_in['B_up'], 'L0_cond_A_down': _L0_cond_in['A_down'], 'L0_cond_B_down': _L0_cond_in['B_down'], 'L0_ffn_gate_qweight': _L0_ffn_in['gate_qweight'], 'L0_ffn_gate_scales': _L0_ffn_in['gate_scales'], 'L0_ffn_gate_zeros': _L0_ffn_in['gate_zeros'], 'L0_ffn_up_qweight': _L0_ffn_in['up_qweight'], 'L0_ffn_up_scales': _L0_ffn_in['up_scales'], 'L0_ffn_up_zeros': _L0_ffn_in['up_zeros'], 'L0_ffn_down_qweight': _L0_ffn_in['down_qweight'], 'L0_ffn_down_scales': _L0_ffn_in['down_scales'], 'L0_ffn_down_zeros': _L0_ffn_in['down_zeros'], 'L1_cond_W_sess': _L1_cond_in['W_sess'], 'L1_cond_b_sess': _L1_cond_in['b_sess'], 'L1_cond_W2': _L1_cond_in['W2'], 'L1_cond_b2': _L1_cond_in['b2'], 'L1_ffn_W_base': _L1_ffn_in['W_base'], 'L1_ffn_b_base': _L1_ffn_in['b_base'], 'L1_ffn_W_router': _L1_ffn_in['W_router'], 'L1_ffn_A': _L1_ffn_in['A'], 'L1_ffn_B': _L1_ffn_in['B'], 'L2_cond_weights': _L2_cond_in['weights'], 'L2_ffn_weight_packed': _L2_ffn_in['weight_packed'], 'L2_ffn_weight_scale': _L2_ffn_in['weight_scale'], 'L2_ffn_weight_var_mask': _L2_ffn_in['weight_var_mask'], 'L2_ffn_bias': _L2_ffn_in['bias'], 'L3_cond_weight': _L3_cond_in['weight'], 'L3_ffn_W': _L3_ffn_in['W'], 'L3_ffn_b': _L3_ffn_in['b'], 'L3_ffn_A': _L3_ffn_in['A'], 'L3_ffn_B': _L3_ffn_in['B'], 'L3_ffn_gate_w': _L3_ffn_in['gate_w'], 'L3_ffn_gate_b': _L3_ffn_in['gate_b']}

def reference(x, itok_B_2_6, itok_B_0_7, itok_B_2182_4065, itok_B_0_15, itok_B_3_7, _lenS, L0_cond_W_gate, L0_cond_W_up, L0_cond_W_down, L0_cond_A_gate, L0_cond_B_gate, L0_cond_A_up, L0_cond_B_up, L0_cond_A_down, L0_cond_B_down, L0_ffn_gate_qweight, L0_ffn_gate_scales, L0_ffn_gate_zeros, L0_ffn_up_qweight, L0_ffn_up_scales, L0_ffn_up_zeros, L0_ffn_down_qweight, L0_ffn_down_scales, L0_ffn_down_zeros, L1_cond_W_sess, L1_cond_b_sess, L1_cond_W2, L1_cond_b2, L1_ffn_W_base, L1_ffn_b_base, L1_ffn_W_router, L1_ffn_A, L1_ffn_B, L2_cond_weights, L2_ffn_weight_packed, L2_ffn_weight_scale, L2_ffn_weight_var_mask, L2_ffn_bias, L3_cond_weight, L3_ffn_W, L3_ffn_b, L3_ffn_A, L3_ffn_B, L3_ffn_gate_w, L3_ffn_gate_b):
    import jax
    import jax.numpy as jnp

    def _L0_cond_ref(x, W_gate, W_up, W_down, A_gate, B_gate, A_up, B_up, A_down, B_down, lora_indices, layer_idx):
        import jax, jax.numpy as jnp
        import numpy as np
        B, N, H, F = (4, 64, 512, 1376)
        L, R, RANK = (1, 16, 16)
        SCALE = 0.5

        def lora_add(base, inp, A, B):
            Ab = A[layer_idx][lora_indices]
            Bb = B[layer_idx][lora_indices]
            t = jnp.einsum('bri,bni->bnr', Ab, inp)
            return base + jnp.einsum('bor,bnr->bno', Bb, t) * SCALE
        gate = lora_add(jnp.einsum('bnh,fh->bnf', x, W_gate), x, A_gate, B_gate)
        up = lora_add(jnp.einsum('bnh,fh->bnf', x, W_up), x, A_up, B_up)
        act = jax.nn.silu(gate) * up
        down = lora_add(jnp.einsum('bnf,hf->bnh', act, W_down), act, A_down, B_down)
        return down

    def _L0_ffn_ref(x, gate_qweight, gate_scales, gate_zeros, up_qweight, up_scales, up_zeros, down_qweight, down_scales, down_zeros):
        import jax, jax.numpy as jnp
        import numpy as np
        HIDDEN = 512
        INTER = 1376
        GROUPSIZE = 128
        PACK = 8

        def dequant_gptq(qweight, scales, zeros, groupsize):
            K = qweight.shape[0] * PACK
            N = qweight.shape[1]
            k = jnp.arange(K)
            q = qweight[k // PACK, :] >> (k % PACK * 4)[:, None] & 15
            n = jnp.arange(N)
            z = zeros[:, n // PACK] >> (n % PACK * 4)[None, :] & 15
            s = scales.astype(jnp.float32)
            zp = (z.astype(jnp.float32) + 1.0) * s
            g = k // groupsize
            return q.astype(jnp.float32) * s[g] - zp[g]
        B, S, H = x.shape
        x2 = x.reshape(-1, H).astype(jnp.float32)
        Wg = dequant_gptq(gate_qweight, gate_scales, gate_zeros, GROUPSIZE)
        Wu = dequant_gptq(up_qweight, up_scales, up_zeros, GROUPSIZE)
        Wd = dequant_gptq(down_qweight, down_scales, down_zeros, GROUPSIZE)
        gate = x2 @ Wg
        up = x2 @ Wu
        inter = gate * jax.nn.sigmoid(gate) * up
        out = (inter @ Wd).astype(jnp.float16)
        return out.reshape(B, S, H)

    def _L1_cond_ref(x, session_ids, channel_counts, seq_lens, W_sess, b_sess, W2, b2):
        import jax, jax.numpy as jnp
        import numpy as np
        SESSION_CHANNELS = [128, 160, 192, 224, 240, 248, 252, 32]
        N_SESS = len(SESSION_CHANNELS)
        B, MAX_C, MAX_T = (16, 32, 512)
        HID, N_SRC = (64, 32)
        cmask = (jnp.arange(x.shape[1])[None, :] < channel_counts[:, None]).astype(x.dtype)
        xm = x * cmask[:, :, None]
        W = W_sess[session_ids]
        b = b_sess[session_ids]
        h = jnp.einsum('bct,bch->bht', xm, W) + b[:, :, None]
        h = jax.nn.gelu(h, approximate=False)
        out = jnp.einsum('bht,hs->bst', h, W2) + b2[None, :, None]
        tmask = (jnp.arange(x.shape[2])[None, :] < seq_lens[:, None]).astype(x.dtype)
        return out * tmask[:, None, :]

    def _L1_ffn_ref(x, W_base, b_base, W_router, A, B):
        import jax, jax.numpy as jnp
        import numpy as np
        NUM_EXPERTS = 8
        TOP_K = 2
        RANK = 16
        LORA_ALPHA = 32
        SCALING = LORA_ALPHA / RANK
        bs, seq, d_in = x.shape
        T = bs * seq
        xf = x.reshape(T, d_in)
        base = xf @ W_base.T + b_base
        logits = xf @ W_router.T
        rw, sel = jax.lax.top_k(logits, TOP_K)
        rw = jax.nn.softmax(rw, axis=-1)
        onehot = jax.nn.one_hot(sel, NUM_EXPERTS, dtype=rw.dtype)
        w = jnp.einsum('tk,tke->te', rw, onehot)
        h = jnp.einsum('td,erd->ter', xf, A)
        lora = jnp.einsum('ter,te,eor->to', h, w, B) * SCALING
        return (base + lora).reshape(bs, seq, -1)

    def _L2_cond_ref(x, weights, condition):
        import jax, jax.numpy as jnp
        import numpy as np
        NUM_CONDITIONS = 16
        IN_CH = 32
        OUT_CH = 32
        B = 64
        T = 512
        W = weights[condition]
        return jnp.einsum('bct,bcd->bdt', x, W)

    def _L2_ffn_ref(x, weight_packed, weight_scale, weight_var_mask, bias):
        import jax, jax.numpy as jnp
        import numpy as np

        def _block_dequantize_mixed(packed, scale, mask):
            q_lo = packed & 15
            q_hi = packed >> 4 & 15
            q = jnp.stack([q_lo, q_hi], axis=-1).reshape(packed.shape[0], -1)
            scale_eff = scale.astype(jnp.float32) * jnp.where(mask[:, None], 1.0, 0.5)
            return (q.astype(jnp.float32) - 8.0) * scale_eff
        out_features = bias.shape[0]
        in_features = x.shape[-1]
        w = _block_dequantize_mixed(weight_packed, weight_scale, weight_var_mask)
        w = w.reshape(out_features, in_features)
        return jnp.einsum('bsi,oi->bso', x, w) + bias

    def _L3_cond_ref(x, weight, adapter_ids):
        import jax, jax.numpy as jnp
        import numpy as np
        MAX_LORAS, OUT, IN = (8, 512, 512)
        B, S = (4, 256)
        w = weight[adapter_ids]
        return jnp.einsum('bsi,boi->bso', x, w)

    def _L3_ffn_ref(hidden_states, W, b, A, B, gate_w, gate_b):
        import jax, jax.numpy as jnp
        import numpy as np
        RANKS = (8, 16, 32, 64)
        TOPK = 1
        SCALING = 1.0 / 4
        bsz, seq, d_in = hidden_states.shape
        out = jnp.einsum('bsd,od->bso', hidden_states, W) + b
        x = hidden_states.reshape(-1, d_in)
        scores = x @ gate_w.T + gate_b
        probs = jax.nn.softmax(scores, axis=-1)
        routing_weights, selected = jax.lax.top_k(probs, TOPK)
        routing_weights = routing_weights / jnp.sum(routing_weights, axis=-1, keepdims=True)
        lora_outputs = jnp.stack([x @ A[:r, :].T @ B[:, :r].T for r in RANKS], axis=1)
        sel = jnp.take_along_axis(lora_outputs, selected[:, :, None], axis=1)
        final = jnp.sum(sel * routing_weights[:, :, None], axis=1)
        return out + final.reshape(bsz, seq, -1)
    x = x + _L0_ffn_ref(_L0_cond_ref(x, L0_cond_W_gate, L0_cond_W_up, L0_cond_W_down, L0_cond_A_gate, L0_cond_B_gate, L0_cond_A_up, L0_cond_B_up, L0_cond_A_down, L0_cond_B_down, itok_B_2_6, 0), L0_ffn_gate_qweight, L0_ffn_gate_scales, L0_ffn_gate_zeros, L0_ffn_up_qweight, L0_ffn_up_scales, L0_ffn_up_zeros, L0_ffn_down_qweight, L0_ffn_down_scales, L0_ffn_down_zeros)
    x = x + _L1_ffn_ref(_L1_cond_ref(x, itok_B_0_7, _lenS, itok_B_2182_4065, L1_cond_W_sess, L1_cond_b_sess, L1_cond_W2, L1_cond_b2), L1_ffn_W_base, L1_ffn_b_base, L1_ffn_W_router, L1_ffn_A, L1_ffn_B)
    x = x + _L2_ffn_ref(_L2_cond_ref(x, L2_cond_weights, itok_B_0_15), L2_ffn_weight_packed, L2_ffn_weight_scale, L2_ffn_weight_var_mask, L2_ffn_bias)
    x = x + _L3_ffn_ref(_L3_cond_ref(x, L3_cond_weight, itok_B_3_7), L3_ffn_W, L3_ffn_b, L3_ffn_A, L3_ffn_B, L3_ffn_gate_w, L3_ffn_gate_b)
    return x

_drawn_inputs = setup_inputs


def setup_inputs(seed=0):
    import zlib

    import numpy as np

    out = dict(_drawn_inputs(seed))
    spreads = {}
    factors = {'L1_cond_b_sess': 8.0,
     'L1_cond_b2': 8.0,
     'L1_ffn_b_base': 27.899,
     'L1_ffn_W_router': 8.0,
     'L1_ffn_A': 8.0,
     'L1_ffn_B': 8.0,
     'L3_ffn_b': 59.701,
     'L3_ffn_A': 3.171,
     'L3_ffn_B': 3.088,
     'L3_ffn_gate_w': 3.712,
     'L3_ffn_gate_b': 37.537}
    for name, (base, spread) in spreads.items():
        noise = np.random.default_rng([zlib.crc32(name.encode()), seed]).standard_normal(out[name].shape)
        drawn = base * np.exp(spread * noise) if base else spread * noise
        out[name] = jnp.asarray(drawn.astype(out[name].dtype))
    for name, factor in factors.items():
        out[name] = (out[name] * factor).astype(out[name].dtype)
    return out
```

```python
import numpy as np
from contextlib import ExitStack

import concourse.bass as bass
from concourse import mybir

ALU = mybir.AluOpType
ACT = mybir.ActivationFunctionType
AX_X = mybir.AxisListType.X
F32 = mybir.dt.float32
F16 = mybir.dt.float16
I32 = mybir.dt.int32
U32 = mybir.dt.uint32
U8 = mybir.dt.uint8

P = 128
B, S, H = 128, 32, 512
TOK = B * S
KH = H // P
FF = 1376
NF = -(-FF // P)
FP = NF * P
RANK, ADAPT = 16, 16

WS = 256.0
IWS = 1.0 / WS

GU = NF * 2 * KH * P
DN = NF * H
WFLAT = GU + DN

TA = 256
NA = TOK // TA
BA = TA // S
assert BA * RANK == P
LA = (2 * KH + NF) * RANK
LB = 2 * FP + H
NIX = BA + 1
DQ = WFLAT // NA
assert DQ * NA == WFLAT and DQ % 8 == 0

TB = 512
NB = TOK // TB


GB = 4
NG = B // GB
HID = 64
NSESS, NCOND = 8, 16
EXP, R1 = 8, 16
WAR = EXP * R1 + EXP
AD3 = 8
NCH = (B + AD3 * (GB - 1)) // GB
R3, NR3 = 64, 4
WAG = R3 + NR3
NO_ROW = 2 * TOK

LATE_B = [("base1", KH * H), ("ar1", KH * WAR), ("b1", H), ("mix1", 2 * S)]
LATE_C = [("base3", KH * H), ("ag3", KH * WAG), ("b3", H)]
NLB, NLC = sum(n for _, n in LATE_B), sum(n for _, n in LATE_C)
NLW = AD3 * KH * H
NLATE = NLB + NLC + NLW
LQ = NLATE // NB
DQ2 = KH * H // NB
assert LQ * NB == NLATE

CONSTS = {}
for _name, _n in (("col", 1), ("mod16", 1), ("mod32", 1), ("hcol", KH), ("iota8", 8), ("sign", 2), ("one", 2),
                  ("level", R3), ("blocks", GB), ("batch1", B), ("before", B), ("slot", NCH), ("ones", P),
                  ("ident", P), ("own_batch", TA)):
    CONSTS[_name] = (sum(n for _, n in CONSTS.values()), _n)
NCONST = sum(n for _, n in CONSTS.values())
BIASES = {}
for _name, _n in (("mix1", S), ("base1", H), ("ffn2", H), ("base3", H), ("gate3", NR3)):
    BIASES[_name] = (sum(n for _, n in BIASES.values()), _n)
NBIAS = sum(n for _, n in BIASES.values())
IDS = {}
for _name, _n in (("lora0", B), ("lora0_own", NA), ("sess_own", NG), ("cond_own", NG), ("len_own", NG),
                  ("sess", B), ("seq", B), ("adapter", B), ("adapter_own", 1)):
    IDS[_name] = (sum(n for _, n in IDS.values()), _n)
NIDS = sum(n for _, n in IDS.values())


class Arena:

    def __init__(self, tensor):
        self.tensor, self.at, self.top = tensor, 0, 0

    def take(self, n, dtype):
        size = n * (2 if dtype == F16 else 4)
        start = self.at
        self.at += (size + 31) // 32 * 32
        self.top = max(self.top, self.at)
        ap = self.tensor[:, start // 2:(start + size) // 2]
        return ap if dtype == F16 else ap.bitcast(dtype)


def mm3(pe, out, a, b, start, stop):
    pe.matmul(out, a[0], b[0], start=start, stop=False)
    pe.matmul(out, a[0], b[1], start=False, stop=False)
    return pe.matmul(out, a[1], b[0], start=False, stop=stop)


def program(nc, d, out):
    ctx = ExitStack()
    with ctx:
        def psum(name):
            return ctx.enter_context(nc.psum_tensor(name, [P, 512], F32))

        def sem(name):
            return ctx.enter_context(nc.semaphore(name))

        room = Arena(ctx.enter_context(nc.sbuf_tensor("room", [P, 207 * 512], F16)))
        bank = [psum(f"bank{n}") for n in range(8)]

        def scratch(name, shape, dtype):
            return nc.dram_tensor(name, shape, dtype).ap()
        lora_a = scratch("lora_a", (ADAPT * P, 2 * LA), F16)
        lora_b = scratch("lora_b", (ADAPT * RANK, 2 * LB), F16)
        c0 = scratch("c0", (2, P, KH, TOK), F16)
        wq = scratch("wq", (2, P, WFLAT), F16)

        late = scratch("late", (2, P, NLATE), F16)
        x1 = scratch("x1", (TOK, H), F32)
        x3 = scratch("x3", (TOK, H), F32)

        w0 = [room.take(WFLAT, F16) for _ in range(2)]
        wgu = [w[:, 0:GU].rearrange("p (f g k c) -> p f g k c", f=NF, g=2, k=KH) for w in w0]
        wdn = [w[:, GU:WFLAT].rearrange("p (f c) -> p f c", f=NF) for w in w0]
        consts = room.take(NCONST, F32)
        biases = room.take(NBIAS, F32)
        ids = room.take(NIDS, I32)

        def const(name):
            return consts[:, CONSTS[name][0]:CONSTS[name][0] + CONSTS[name][1]]

        def bias_of(name):
            return biases[:, BIASES[name][0]:BIASES[name][0] + BIASES[name][1]]

        def ids_of(name):
            return ids[:, IDS[name][0]:IDS[name][0] + IDS[name][1]]

        own_batch = const("own_batch")
        shift = room.take(8, I32)
        index1 = room.take(2 * NG, I32)
        clen = room.take(NG, F32)
        tmask = room.take(KH * B, F32).rearrange("p (k b) -> p k b", k=KH)
        bias_hid = room.take(B // 2, F32)
        rows_in = room.take(NCH, I32)
        rows_out = room.take(NCH, I32)
        adapter = room.take(NCH, I32)
        index = room.take(NA * NIX, I32)
        index_f = room.take(NA * NIX, F32)
        stage_start = room.at

        prep_out_start = room.at
        la = [room.take(BA * 2 * LA, F16) for _ in range(2)]
        la_raw = room.take(BA * 2 * LA, F16)
        lb = [room.take(2 * LB, F16) for _ in range(2)]
        index_now = [room.take(NIX, I32) for _ in range(2)]
        xs = room.take(KH * TA, F32)
        xt = [[room.take(KH * TA, F16) for _ in range(2)] for _ in range(2)]
        prep_in_start = room.at
        act = [room.take(NF * TA, F16).rearrange("p (f t) -> p f t", f=NF) for _ in range(2)]
        sil = [room.take(TA, F32) for _ in range(2)]
        prod = [room.take(TA, F32) for _ in range(2)]
        tf = room.take(TA, F32)
        t_part = [[room.take(TA, F16) for _ in range(2)] for _ in range(3)]
        c0_part = [room.take(KH * TA, F16).rearrange("p (k t) -> p k t", k=KH) for _ in range(2)]
        tables_start = room.at
        dq_q = room.take(DQ, I32)
        dq_zp = room.take(DQ // 8, I32)
        dq_z = room.take(DQ, I32)
        dq_s = room.take(DQ, F16)
        dq_n = room.take(DQ, F32)
        dq_w = room.take(DQ, F32)
        dq_part = [room.take(DQ, F16) for _ in range(2)]
        tables_end = room.at
        PREP = 1664
        RING = 2
        table_room = Arena(room.tensor)
        table_room.at = tables_start
        b_sess = table_room.take(P, F32)
        ids_f = table_room.take(NIDS, F32)
        onehot = table_room.take(B, F32)
        later = table_room.take(B, F32)
        same = table_room.take(B, F32)
        count = table_room.take(4, F32)
        count_i = table_room.take(4, I32)
        spread = table_room.take(P, F32)
        place = table_room.take(B, F32)
        junk = [table_room.take(B, F32) for _ in range(2)]
        at_place = table_room.take(NCH, F32)
        at_adapter = table_room.take(NCH, F32)
        row_f = table_room.take(NCH, F32)
        empty = table_room.take(NCH, F32)
        row1_f = table_room.take(2 * NG, F32)
        assert table_room.at <= tables_end
        room.at = prep_in_start
        prep_in = [room.take(PREP, F32) for _ in range(RING)]
        room.at = prep_out_start
        prep_out = [[room.take(PREP, F16) for _ in range(2)] for _ in range(RING)]

        room.at = stage_start
        wb_part = [room.take(NLB, F16) for _ in range(2)]
        w2_part = [room.take(KH * H, F16) for _ in range(2)]
        mix1 = room.take(NG * HID, F32)
        mix2 = room.take(NG * S, F32)
        b_start = room.at
        late_in = room.take(LQ, F32)
        late_part = [room.take(LQ, F16) for _ in range(2)]
        p2_in = room.take(DQ2, I32)
        s2_in = room.take(DQ2, F16)
        m2_in = room.take(DQ2 // 2, F16).bitcast(U8)[:, 0:DQ2]
        n2 = room.take(DQ2, F32)
        e2 = room.take(DQ2, F32)
        ct = [[room.take(KH * TB, F16).rearrange("p (k t) -> p k t", k=KH) for _ in range(2)] for _ in range(2)]
        act2 = [room.take(NF * TB, F16).rearrange("p (f t) -> p f t", f=NF) for _ in range(2)]
        sil2 = [room.take(TB, F32) for _ in range(2)]
        prod2 = [room.take(TB, F32) for _ in range(2)]
        xn = [room.take(4 * H, F32).rearrange("p (g h) -> p g h", g=4) for _ in range(2)]
        out16 = [room.take(H, F16) for _ in range(2)]

        room.at = b_start
        wc_part = [room.take(NLC, F16) for _ in range(2)]
        c_start = room.at

        def ring(n, size, dtype=F16, parts=0):
            if parts:
                return [[room.take(size, dtype) for _ in range(parts)] for _ in range(n)]
            return [room.take(size, dtype) for _ in range(n)]

        x1_in = ring(2, H, F32)
        x1_part = ring(2, H, parts=2)
        x1b = ring(4, H, F32)
        bd1_f = room.take(GB * HID, F32)
        bd1 = ring(2, GB * HID, parts=2)
        bd2_f = room.take(GB * S, F32)
        bd2 = ring(2, GB * S, parts=2)
        hid_f = ring(2, H, F32)
        hid = [ring(2, H, parts=2) for _ in range(2)]
        c1_f = room.take(KH * P, F32)
        c1 = ring(2, KH * P, parts=2)
        lg = room.take(8, F32)
        mx8 = room.take(8, F32)
        ix8 = room.take(8, U32)
        gap = room.take(8, F32)
        th = room.take(8, F32)
        ixf = room.take(8, F32)
        pp = room.take(8, F32)
        e1x = [room.take(8, F32) for _ in range(3)]
        hw = room.take(P, F32)
        hwt = [room.take(P, F16) for _ in range(2)]
        x2_f = ring(2, H, F32)
        x2_part = ring(2, H, parts=2)
        x2b = ring(2, H, F32)
        c2 = ring(2, KH * P, parts=2)
        x3_f = ring(2, H, F32)
        room.at = c_start
        x3_in = ring(4, H, F32)
        x3b = ring(4, H, F32)
        row_now = [room.take(8, I32) for _ in range(4)]
        row_put = [room.take(8, I32) for _ in range(2)]
        x3t = ring(2, KH * P, parts=2)
        c3_f = ring(2, H, F32)
        c3t = ring(2, KH * P, parts=2)
        sc8 = room.take(8, F32)
        mc8 = room.take(8, F32)
        ic8 = room.take(8, U32)
        icf = room.take(8, F32)
        negm = room.take(8, F32)
        ex = room.take(8, F32)
        esum = room.take(8, F32)
        rec = room.take(8, F32)
        wn = room.take(8, F32)
        keep = room.take(R3, F32)
        hl = room.take(P, F32)
        hlt = [room.take(P, F16) for _ in range(2)]
        fin = ring(2, H, F32)
        w3 = [w[:, 0:NLW].rearrange("p (a k c) -> p a k c", a=AD3, k=KH) for w in w0]

        def late_weight(parts, table, name, k):
            at = sum(n for _, n in table[:[m for m, _ in table].index(name)])
            size = dict(table)[name]
            return [w[:, at:at + size].rearrange("p (k c) -> p k c", k=k) for w in parts]

        w_base1 = late_weight(wb_part, LATE_B, "base1", KH)
        w_ar1 = late_weight(wb_part, LATE_B, "ar1", KH)
        w_b1 = late_weight(wb_part, LATE_B, "b1", 1)
        w_mix1 = late_weight(wb_part, LATE_B, "mix1", 1)
        w_2 = [w.rearrange("p (k c) -> p k c", k=KH) for w in w2_part]
        w_base3 = late_weight(wc_part, LATE_C, "base3", KH)
        w_ag3 = late_weight(wc_part, LATE_C, "ag3", KH)
        w_b3 = late_weight(wc_part, LATE_C, "b3", 1)

        const_in = sem("const_in")
        index_ready = sem("index_ready")
        prep_loaded = [sem(f"prep_loaded{n}") for n in range(RING)]
        prep_hi = sem("prep_hi")
        prep_lo = sem("prep_lo")
        table_stored = [sem(f"table_stored{n}") for n in range(RING)]
        x_loaded = sem("x_loaded")
        pool_turns = sem("pool_turns")
        dve_turns = sem("dve_turns")
        x_hi = sem("x_hi")
        x_split = sem("x_split")
        index_copied = sem("index_copied")
        la_loaded = sem("la_loaded")
        la_ready = sem("la_ready")
        lb_loaded = [sem(f"lb_loaded{n}") for n in range(2)]
        gate_ready = sem("gate_ready")
        up_ready = sem("up_ready")
        silu_done = sem("silu_done")
        prod_done = sem("prod_done")
        act_hi = sem("act_hi")
        act_split = sem("act_split")
        t_ready = sem("t_ready")
        t_step = sem("t_step")
        t_split = sem("t_split")
        down_ready = sem("down_ready")
        c0_hi = sem("c0_hi")
        c0_split = sem("c0_split")
        c0_stored = sem("c0_stored")
        dq_loaded = sem("dq_loaded")
        dq_bits = sem("dq_bits")
        dq_step = sem("dq_step")
        dq_split = sem("dq_split")
        wq_stored = sem("wq_stored")
        wq_loaded = [sem(f"wq_loaded{n}") for n in range(NF + 1)]
        ct_loaded = [sem(f"ct_loaded{n}") for n in range(2)]
        xn_loaded = [sem(f"xn_loaded{n}") for n in range(2)]
        gate2_ready = sem("gate2_ready")
        up2_ready = sem("up2_ready")
        silu2_done = sem("silu2_done")
        prod2_done = sem("prod2_done")
        act2_hi = sem("act2_hi")
        act2_split = sem("act2_split")
        down2_ready = sem("down2_ready")
        out16_done = sem("out16_done")
        x1_done = sem("x1_done")
        x1_stored = [sem(f"x1_stored{n}") for n in range(2)]

        table_step = sem("table_step")
        table_mm = sem("table_mm")
        late_loaded = sem("late_loaded")
        late_free = sem("late_free")
        late_hi = sem("late_hi")
        late_split = sem("late_split")
        late_stored = sem("late_stored")
        deq2_loaded = sem("deq2_loaded")
        deq2_step = sem("deq2_step")
        deq2_done = sem("deq2_done")
        mix_loaded = sem("mix_loaded")
        mix_ready = sem("mix_ready")
        wb_loaded = sem("wb_loaded")
        wc_loaded = sem("wc_loaded")
        w3_loaded = sem("w3_loaded")
        x1b_done = sem("x1b_done")
        p_step = sem("p_step")
        x1_split = sem("x1_split")
        bd1_ready = sem("bd1_ready")
        bd2_ready = sem("bd2_ready")
        hid_ready = sem("hid_ready")
        gelu_done = sem("gelu_done")
        hid_hi = sem("hid_hi")
        hid_split = sem("hid_split")
        mixed_ready = sem("mixed_ready")
        c1_step = sem("c1_step")
        c1_split = sem("c1_split")
        router_ready = sem("router_ready")
        r_step = sem("r_step")
        gap_ready = sem("gap_ready")
        tanh_done = sem("tanh_done")
        hw_done = sem("hw_done")
        hwt_ready = sem("hwt_ready")
        hwt_hi = sem("hwt_hi")
        hwt_split = sem("hwt_split")
        x2_ready = sem("x2_ready")
        x2_done = sem("x2_done")
        x2_hi = sem("x2_hi")
        x2_split = sem("x2_split")
        x2b_done = sem("x2b_done")
        c2_ready = sem("c2_ready")
        c2_hi = sem("c2_hi")
        c2_split = sem("c2_split")
        y3_ready = sem("y3_ready")
        x3_done = sem("x3_done")
        row_copied = sem("row_copied")
        row_put_copied = sem("row_put_copied")
        x3b_done = sem("x3b_done")
        xt3_ready = sem("xt3_ready")
        xt3_hi = sem("xt3_hi")
        xt3_split = sem("xt3_split")
        cond3_ready = sem("cond3_ready")
        c3_done = sem("c3_done")
        ct3_ready = sem("ct3_ready")
        ct3_hi = sem("ct3_hi")
        ct3_split = sem("ct3_split")
        ag3_ready = sem("ag3_ready")
        g_step = sem("g_step")
        negm_ready = sem("negm_ready")
        exp_done = sem("exp_done")
        hl_done = sem("hl_done")
        hlt_ready = sem("hlt_ready")
        hlt_hi = sem("hlt_hi")
        hlt_split = sem("hlt_split")
        fin_ready = sem("fin_ready")
        fin_done = sem("fin_done")
        x1_loaded = [sem(f"x1_loaded{n}") for n in range(2)]
        x3_stored = [sem(f"x3_stored{n}") for n in range(2)]
        x3_loaded = [sem(f"x3_loaded{n}") for n in range(4)]
        fin_stored = [sem(f"fin_stored{n}") for n in range(2)]

        jobs = []
        la_in = d["lora_a"].rearrange("(a p) c -> p a c", p=P)
        la_out = lora_a.rearrange("(a p) c -> p a c", p=P)
        for j in range(4):
            q = len(jobs) % RING
            w = 4 * LA
            jobs.append((la_in[:, 4 * j:4 * j + 4, :], w, prep_out[q][0][:, 0:w], prep_out[q][1][:, 0:w],
                         [(la_out[:, 4 * j:4 * j + 4, h * LA:(h + 1) * LA],
                           prep_out[q][h][:, 0:w].rearrange("p (a c) -> p a c", a=4)) for h in range(2)]))
        for r in range(2):
            for j in range(2):
                q = len(jobs) % RING
                jobs.append((d["lora_b"][r * P:(r + 1) * P, j * PREP:(j + 1) * PREP], PREP,
                             prep_out[q][0], prep_out[q][1],
                             [(lora_b[r * P:(r + 1) * P, h * LB + j * PREP:h * LB + (j + 1) * PREP],
                               prep_out[q][h]) for h in range(2)]))
        tables = len(jobs)
        assert 2 * PREP == LB
        chunk = 2 * KH * P
        for at in range(0, WFLAT, chunk):
            w = min(chunk, WFLAT - at)
            jobs.append((d["w_cond"][:, at:at + w], w, w0[0][:, at:at + w], w0[1][:, at:at + w], []))

        def jobs_for(flat_end):
            return tables + -(-flat_end // chunk)

        CR_PROD = 2
        CR_DOWN = 8
        CR_C0 = 2
        CR_X = 1
        CR_PREP = RING

        block = ctx.enter_context(nc.Block())

        def valid(i, first, end):
            return not isinstance(i, int) or first <= i < end

        def run_b(eng, step):
            turns = (NG - 2 - 3) // 4
            for i in range(-2, 3):
                step(i, i % 4)
            with eng.Fori(0, turns) as it:
                for u in range(3, 7):
                    step(it * 4 + u, u % 4)
            for i in range(4 * turns + 3, NG + 1):
                step(i, i % 4)

        def run_c(eng, step):
            turns = (NCH - 5 - 2) // 4
            for i in range(-5, 2):
                step(i, i % 4)
            with eng.Fori(0, turns) as it:
                for u in range(2, 6):
                    step(it * 4 + u, u % 4)
            for i in range(4 * turns + 2, NCH):
                step(i, i % 4)

        def slot_count(g, v, ring_size):
            return (g - v % ring_size) * (16 // ring_size) + 16

        def load_count(g, v):
            return slot_count(g, v, 2)

        def p_steps(g, n):
            if n <= 3:
                return g * 5 - 4 + n if not isinstance(g, int) or g >= 2 else g * 3 + n
            if isinstance(g, int) and g + 2 >= NG:
                return (NG - 1) * 5 - 4 + 3 + 2 + (g + 2 - NG) * 2
            return (g + 2) * 5 - 4 + 3

        def load_beside(sp, i):
            sp.wait_ge(late_split, i + 1)
            sp.dma_start(late_in, d["late"][:, bass.ds(i * LQ, LQ)]).then_inc(late_loaded, 16)
            sp.wait_ge(deq2_done, i + 1)
            for dst, name in ((p2_in, "p2"), (s2_in, "s2"), (m2_in, "m2")):
                sp.dma_start(dst, d[name][:, bass.ds(i * DQ2, DQ2)]).then_inc(deq2_loaded, 16)

        def load_ct(sp, i, p):
            for h in range(2):
                sp.dma_start(ct[p][h], c0[h][:, :, bass.ds(i * TB, TB)]).then_inc(ct_loaded[p], 16)

        def load_xn(sp, i, p):
            xn_in = d["x"].rearrange("(g p) h -> p g h", p=P)
            sp.dma_start(xn[p], xn_in[:, bass.ds(i * 4, 4), :]).then_inc(xn_loaded[p], 16)

        @block.sync
        def _(sp):
            sp.dma_start(consts, d["consts"]).then_inc(const_in, 16)
            sp.dma_start(shift, d["shift"]).then_inc(const_in, 16)
            sp.dma_start(ids, d["ids"]).then_inc(const_in, 16)
            sp.dma_start(biases, d["biases"]).then_inc(const_in, 16)
            sp.dma_start(b_sess, d["b_sess"]).then_inc(const_in, 16)
            for n, (src, w, _, _, _) in enumerate(jobs):
                sp.wait_ge(prep_lo, n - RING + 1) if n >= RING else None
                dst = prep_in[n % RING][:, 0:w]
                if len(src.shape) == 3:
                    dst = dst.rearrange("p (a c) -> p a c", a=src.shape[1])
                sp.dma_start(dst, src).then_inc(prep_loaded[n % RING], 16)
            xt_in = d["xt"].rearrange("(k p) t -> p k t", p=P)
            with sp.Fori(0, NA) as i:
                sp.wait_ge(x_split, i + 1)
                sp.dma_start(xs.rearrange("p (k t) -> p k t", k=KH),
                             xt_in[:, :, bass.ds(i * TA, TA)]).then_inc(x_loaded, 16)
                sp.wait_ge(dq_split, i + 1)
                sp.dma_start(dq_q, d["q"][:, bass.ds(i * DQ, DQ)]).then_inc(dq_loaded, 16)
                sp.dma_start(dq_zp, d["z"][0:1, bass.ds(i * (DQ // 8), DQ // 8)].partition_broadcast(P)
                             ).then_inc(dq_loaded, 16)
                sp.dma_start(dq_s, d["s"][0:1, bass.ds(i * DQ, DQ)].partition_broadcast(P)).then_inc(dq_loaded, 16)
            sp.wait_ge(down_ready, 4 * NA + CR_DOWN)
            sp.wait_ge(wq_stored, 32 * NA)
            for f in range(NF):
                for h in range(2):
                    sp.dma_start(w0[h][:, f * chunk:(f + 1) * chunk],
                                 wq[h, :, f * chunk:(f + 1) * chunk]).then_inc(wq_loaded[f], 16)
                if f == 0:
                    sp.wait_ge(c0_stored, 32 * NA + 32)
                    load_ct(sp, 0, 0)
            for h in range(2):
                sp.dma_start(w0[h][:, GU:WFLAT], wq[h, :, GU:WFLAT]).then_inc(wq_loaded[NF], 16)
            load_beside(sp, 0)
            load_xn(sp, 0, 0)
            load_ct(sp, 1, 1)
            load_xn(sp, 1, 1)
            load_beside(sp, 1)
            with sp.Fori(1, NB // 2) as it:
                for p in range(2):
                    sp.wait_ge(down2_ready, (it * 2 + p - 1) * 4)
                    load_ct(sp, it * 2 + p, p)
                    load_beside(sp, it * 2 + p)
                    sp.wait_ge(x1_stored[p], it * 64)
                    load_xn(sp, it * 2 + p, p)
            sp.wait_ge(late_stored, 32 * NB)
            for h in range(2):
                sp.dma_start(wb_part[h], late[h, :, 0:NLB]).then_inc(wb_loaded, 16)
            for s in x1_stored:
                sp.wait_ge(s, 64 * NB // 2)
            for g in range(2):
                sp.dma_start(x1_in[g], x1[g * P:(g + 1) * P, :]).then_inc(x1_loaded[g], 16)
            sp.wait_ge(down2_ready, 4 * NB)
            for h in range(2):
                sp.dma_start(wc_part[h], late[h, :, NLB:NLB + NLC]).then_inc(wc_loaded, 16)
                sp.dma_start(w0[h][:, 0:NLW], late[h, :, NLB + NLC:NLATE]).then_inc(w3_loaded, 16)

            def step_b(i, u):
                if valid(i + 3, 2, NG):
                    sp.wait_ge(x1b_done, i + 2)
                    sp.wait_ge(x1_split, i + 2)
                    sp.dma_start(x1_in[(u + 3) % 2], x1[bass.ds((i + 3) * P, P), :]).then_inc(x1_loaded[(u + 3) % 2], 16)
                if valid(i - 1, 0, NG):
                    sp.wait_ge(x3_done, i)
                    sp.dma_start(x3[bass.ds((i - 1) * P, P), :], x3_f[(u - 1) % 2]).then_inc(x3_stored[(u - 1) % 2], 16)

            run_b(sp, step_b)

        @block.gpsimd
        def _(pool):
            pool.sem_inc(x_split, 1)
            pool.sem_inc(dq_split, 1)
            pool.sem_inc(x1_done, 4)
            pool.sem_inc(late_free, 1)
            pool.wait_ge(index_ready, 1)
            for s in table_stored:
                pool.wait_ge(s, 32 * tables // RING)
            def pool_wait(on, value):
                pool.wait_ge(on, value)
                pool.sem_inc(pool_turns, 1)

            with pool.Fori(0, NA // 2) as it:
                for p in range(2):
                    i = it * 2 + p
                    pool_wait(down_ready, i * 4 + 4)
                    pool_wait(x_loaded, (i + 1) * 16)
                    pool.tensor_copy(xt[p][0], xs).then_inc(x_hi, 1)
                    pool_wait(x_hi, i + 1)
                    pool.tensor_tensor(xt[p][1], xs, xt[p][0], ALU.subtract).then_inc(x_split, 1)
                    pool.tensor_copy(index_now[p], index[:, bass.ds(i * NIX, NIX)]).then_inc(index_copied, 1)
                    pool_wait(index_copied, i + 1)
                    for b in range(BA):
                        pool.indirect_dma_start(
                            la_raw[:, b * 2 * LA:(b + 1) * 2 * LA], None, lora_a,
                            bass.IndirectOffsetOnAxis(ap=index_now[p][:, b:b + 1], axis=0)
                        ).then_inc(la_loaded, 16)
                    pool.indirect_dma_start(
                        lb[p], None, lora_b,
                        bass.IndirectOffsetOnAxis(ap=index_now[p][:, BA:BA + 1], axis=0)
                    ).then_inc(lb_loaded[p], 16)
                    pool_wait(la_loaded, (i + 1) * 16 * BA)
                    pool.tensor_copy(la[p].rearrange("p (c b r) -> p c b r", b=BA, r=RANK),
                                     la_raw.rearrange("p (b c r) -> p c b r", b=BA, r=RANK)).then_inc(la_ready, 1)
                    pool_wait(la_ready, i + 1)
                    pool_wait(dq_bits, (i + 1) * 2)
                    pool.tensor_scalar(dq_n, dq_n, -1.0, WS, ALU.add, ALU.mult).then_inc(dq_step, 1)
                    pool_wait(dq_step, i * 3 + 1)
                    pool.tensor_tensor(dq_w, dq_n, dq_s, ALU.mult).then_inc(dq_step, 1)
                    pool_wait(dq_step, i * 3 + 2)
                    pool.tensor_copy(dq_part[0], dq_w).then_inc(dq_step, 1)
                    pool_wait(dq_step, i * 3 + 3)
                    pool.tensor_tensor(dq_part[1], dq_w, dq_part[0], ALU.subtract).then_inc(dq_split, 1)
                    pool_wait(dq_split, i + 2)
                    for h in range(2):
                        pool.dma_start(wq[h, :, bass.ds(i * DQ, DQ)], dq_part[h]).then_inc(wq_stored, 16)
                    pool_wait(wq_stored, i * 32 + 32)
            pool.wait_ge(down_ready, 4 * NA + CR_DOWN)
            for g in range(NG):
                for n, (dst, width, table) in enumerate(((mix1, HID, d["w_sess"]), (mix2, S, d["w_mix2"]))):
                    pool.indirect_dma_start(
                        dst[:, g * width:(g + 1) * width], None, table,
                        bass.IndirectOffsetOnAxis(ap=index1[:, n * NG + g:n * NG + g + 1], axis=0)
                    ).then_inc(mix_loaded, 16)
            pool.wait_ge(mix_loaded, 32 * NG)
            for g in range(NG):
                v = mix1[:, g * HID:(g + 1) * HID]
                pool.tensor_scalar(v, v, clen[:, g:g + 1], None, ALU.mult)
            pool.tensor_scalar(mix2, mix2, WS, None, ALU.mult).then_inc(mix_ready, 1)
            x1_out = x1.rearrange("(g p) h -> p g h", p=P)
            with pool.Fori(0, NB // 2) as it:
                for p in range(2):
                    i = it * 2 + p
                    pool_wait(late_split, i + 2)
                    for h in range(2):
                        pool.dma_start(late[h, :, bass.ds(i * LQ, LQ)], late_part[h]).then_inc(late_stored, 16)
                    pool_wait(xn_loaded[p], (it + 1) * 16)
                    for g in range(4):
                        pool_wait(out16_done, i * 4 + g + 5)
                        pool.tensor_tensor(xn[p][:, g, :], xn[p][:, g, :], out16[g % 2], ALU.add).then_inc(x1_done, 1)
                        pool_wait(x1_done, i * 4 + g + 5)
                        pool.dma_start(x1_out[:, bass.ds(i * 4 + g, 1), :], xn[p][:, g:g + 1, :]).then_inc(x1_stored[p], 16)
                    pool_wait(late_stored, i * 32 + 32)
                    pool.sem_inc(late_free, 1)
            pool.wait_ge(mix_ready, 1)
            blocks = const("blocks").rearrange("p (q o) -> p q o", o=1)

            def block_diagonal(rows, g, width, f, parts, ready, base):
                row = rows[:, bass.ds(g * width, width)].rearrange("p (o c) -> p o c", o=1)
                pool.tensor_tensor(f.rearrange("p (q c) -> p q c", q=GB), row.broadcast_to((P, GB, width)),
                                   blocks.broadcast_to((P, GB, width)), ALU.mult).then_inc(p_step, 1)
                pool_wait(p_step, base + 1)
                pool.tensor_copy(parts[0], f).then_inc(p_step, 1)
                pool_wait(p_step, base + 2)
                pool.tensor_tensor(parts[1], f, parts[0], ALU.subtract).then_inc(ready, 1)

            def step_b(i, u):
                g, v = i + 2, (u + 2) % 4
                if valid(g, 0, NG):
                    pool_wait(x1_loaded[v % 2], load_count(g, v))
                    if valid(g - 2, 0, NG):
                        pool_wait(hid_ready, 2 * (g - 1))
                    pool.tensor_copy(x1_part[v % 2][0], x1_in[v % 2]).then_inc(p_step, 1)
                    pool_wait(p_step, p_steps(g, 1))
                    pool.tensor_tensor(x1_part[v % 2][1], x1_in[v % 2], x1_part[v % 2][0], ALU.subtract
                                       ).then_inc(x1_split, 1)
                    if valid(g - 4, 0, NG):
                        pool_wait(x2_done, g - 3)
                    pool.tensor_tensor(x1b[v], x1_in[v % 2], bias_of("base1"), ALU.add).then_inc(x1b_done, 1)
                    if valid(g - 1, 0, NG):
                        pool_wait(bd1_ready, g)
                    block_diagonal(mix1, g, HID, bd1_f, bd1[v % 2], bd1_ready, p_steps(g, 1))
                g, v = i, u
                if valid(g, 0, NG):
                    if valid(g - 2, 0, NG):
                        pool_wait(c2_ready, g - 1)
                    if valid(g - 1, 0, NG):
                        pool_wait(bd2_ready, g)
                    block_diagonal(mix2, g, S, bd2_f, bd2[v % 2], bd2_ready, p_steps(g, 4))
                    pool_wait(x2_done, g + 1)
                    pool_wait(x2_hi, g + 1)
                    pool.tensor_tensor(x2_part[v % 2][1], x2_f[v % 2], x2_part[v % 2][0], ALU.subtract
                                       ).then_inc(x2_split, 1)
                    if valid(g - 2, 0, NG):
                        pool_wait(x3_done, g - 1)
                    pool.tensor_tensor(x2b[v % 2], x2_f[v % 2], bias_of("ffn2"), ALU.add).then_inc(x2b_done, 1)

            run_b(pool, step_b)
            for s in x3_stored:
                pool.wait_ge(s, 16 * NG // 2)
            table3 = x3

            def step_c(i, u):
                j, v = i + 5, (u + 5) % 4
                if valid(j, 0, NCH):
                    if valid(j - 4, 0, NCH):
                        pool_wait(xt3_ready, j - 3)
                        pool_wait(x3b_done, j - 3)
                    pool.tensor_copy(row_now[v][:, 0:1], rows_in[:, bass.ds(j, 1)]).then_inc(row_copied, 1)
                    pool_wait(row_copied, j + 1)
                    pool.indirect_dma_start(x3_in[v], None, table3,
                                            bass.IndirectOffsetOnAxis(ap=row_now[v][:, 0:1], axis=0)
                                            ).then_inc(x3_loaded[v], 16)
                j, v = i + 3, (u + 3) % 4
                if valid(j, 0, NCH):
                    pool_wait(x3_loaded[v], slot_count(j, v, 4))
                    if valid(j - 4, 0, NCH):
                        pool_wait(fin_done, j - 3)
                    pool.tensor_tensor(x3b[v], x3_in[v], bias_of("base3"), ALU.add).then_inc(x3b_done, 1)
                j, v = i, u
                if valid(j, 0, NCH):
                    if valid(j - 2, 0, NCH):
                        pool_wait(fin_stored[v % 2], slot_count(j - 2, v, 2))
                    pool.tensor_copy(row_put[v % 2][:, 0:1], rows_out[:, bass.ds(j, 1)]).then_inc(row_put_copied, 1)
                    pool_wait(row_put_copied, j + 1)
                    pool_wait(fin_done, j + 1)
                    pool.indirect_dma_start(out, bass.IndirectOffsetOnAxis(ap=row_put[v % 2][:, 0:1], axis=0),
                                            fin[v % 2], None, bounds_check=TOK - 1, oob_is_err=False
                                            ).then_inc(fin_stored[v % 2], 16)

            run_c(pool, step_c)
            for n in range(2):
                pool.wait_ge(fin_stored[n], 16 * ((NCH + 1 - n) // 2))

        @block.scalar
        def _(act_e):
            act_e.sem_inc(c0_stored, 32)
            act_e.sem_inc(out16_done, 4)
            for n, (_, w, hi, _, stores) in enumerate(jobs):
                act_e.wait_ge(prep_loaded[n % RING], 16 * (n // RING + 1))
                if stores and n >= RING:
                    act_e.wait_ge(table_stored[n % RING], 32 * (n // RING))
                act_e.activation(hi, prep_in[n % RING][:, 0:w], ACT.Copy, scale=WS).then_inc(prep_hi, 1)
                if stores:
                    act_e.wait_ge(prep_lo, n + 1)
                    for dst, src in stores:
                        act_e.dma_start(dst, src).then_inc(table_stored[n % RING], 16)
            with act_e.Fori(0, NA // 2) as it:
                for p in range(2):
                    i = it * 2 + p
                    for f in range(NF):
                        q = (p + f) % 2
                        act_e.wait_ge(gate_ready, i * NF + f + 1)
                        act_e.wait_ge(prod_done, i * NF + f + 1)
                        act_e.activation(sil[q], bank[q][:, 0:TA], ACT.Silu, scale=IWS).then_inc(silu_done, 1)
                    act_e.wait_ge(c0_split, (i + 1) * 4 + CR_C0)
                    for h in range(2):
                        act_e.dma_start(c0[h][:, :, bass.ds(i * TA, TA)], c0_part[h]).then_inc(c0_stored, 16)
            with act_e.Fori(0, NB // 2) as it:
                for p in range(2):
                    i = it * 2 + p
                    for f in range(NF):
                        q = (p + f) % 2
                        act_e.wait_ge(gate2_ready, i * NF + f + 1)
                        act_e.wait_ge(prod2_done, i * NF + f + 1)
                        act_e.activation(sil2[q], bank[q][:, :], ACT.Silu, scale=IWS).then_inc(silu2_done, 1)
                        if f == 3:
                            act_e.wait_ge(late_loaded, i * 16 + 16)
                            act_e.wait_ge(late_free, i + 1)
                            act_e.activation(late_part[0], late_in, ACT.Copy, scale=WS).then_inc(late_hi, 1)
                    for g in range(4):
                        act_e.wait_ge(down2_ready, i * 4 + g + 1)
                        act_e.wait_ge(x1_done, i * 4 + g + 3)
                        act_e.activation(out16[g % 2], bank[4 + g][:, :], ACT.Copy, scale=IWS).then_inc(out16_done, 1)

            def step_b(i, u):
                g, v = i - 1, (u - 1) % 4
                if valid(g, 0, NG):
                    act_e.wait_ge(c2_ready, g + 1)
                    act_e.activation(c2[v % 2][0], bank[6][:, :], ACT.Copy, scale=IWS).then_inc(c2_hi, 1)
                g, v = i, u
                if valid(g, 0, NG):
                    act_e.wait_ge(gap_ready, g + 1)
                    act_e.activation(th[:, 0:1], gap[:, 0:1], ACT.Tanh, scale=0.5).then_inc(tanh_done, 1)
                g, v = i + 2, (u + 2) % 4
                if valid(g, 0, NG):
                    for pair in range(2):
                        act_e.wait_ge(hid_ready, 2 * g + pair + 1)
                        if valid(g - 1, 0, NG):
                            act_e.wait_ge(hid_split, 2 * g + pair - 1)
                        act_e.activation(hid_f[pair], bank[pair][:, :], ACT.Gelu,
                                         bias=bias_hid[:, bass.ds(g * 2 + pair, 1)], scale=IWS).then_inc(gelu_done, 1)
                        act_e.wait_ge(gelu_done, 2 * g + pair + 1)
                        if valid(g - 2, 0, NG):
                            act_e.wait_ge(mixed_ready, g - 1)
                        act_e.activation(hid[v % 2][pair][0], hid_f[pair], ACT.Copy).then_inc(hid_hi, 1)
                g, v = i, u
                if valid(g, 0, NG):
                    act_e.wait_ge(x2_done, g + 1)
                    if valid(g - 2, 0, NG):
                        act_e.wait_ge(c2_ready, g - 1)
                    act_e.activation(x2_part[v % 2][0], x2_f[v % 2], ACT.Copy).then_inc(x2_hi, 1)

            run_b(act_e, step_b)

            def step_c(i, u):
                j, v = i, u
                if valid(j, 0, NCH):
                    act_e.wait_ge(negm_ready, j + 1)
                    act_e.activation(ex[:, 0:NR3], sc8[:, 0:NR3], ACT.Exp, bias=negm[:, 0:1],
                                     accum_out=esum[:, 0:1]).then_inc(exp_done, 1)
                j, v = i + 1, (u + 1) % 4
                if valid(j, 0, NCH):
                    act_e.wait_ge(ct3_ready, j + 1)
                    if valid(j - 2, 0, NCH):
                        act_e.wait_ge(ag3_ready, 2 * (j - 1))
                    act_e.activation(c3t[v % 2][0], bank[2][:, :], ACT.Copy).then_inc(ct3_hi, 1)
                j, v = i + 2, (u + 2) % 4
                if valid(j, 0, NCH):
                    act_e.wait_ge(cond3_ready, j + 1)
                    if valid(j - 2, 0, NCH):
                        act_e.wait_ge(ct3_ready, j - 1)
                    act_e.activation(c3_f[v % 2], bank[1][:, :], ACT.Copy, scale=IWS).then_inc(c3_done, 1)
                j, v = i + 3, (u + 3) % 4
                if valid(j, 0, NCH):
                    act_e.wait_ge(xt3_ready, j + 1)
                    if valid(j - 2, 0, NCH):
                        act_e.wait_ge(cond3_ready, j - 1)
                    act_e.activation(x3t[v % 2][0], bank[0][:, :], ACT.Copy).then_inc(xt3_hi, 1)

            run_c(act_e, step_c)

        @block.vector
        def _(dve):
            dve.sem_inc(prod_done, CR_PROD)
            dve.sem_inc(c0_split, CR_C0)
            dve.sem_inc(prod2_done, CR_PROD)
            dve.sem_inc(late_split, 1)
            dve.sem_inc(deq2_done, 1)
            dve.wait_ge(const_in, 80)
            ix = index_f.rearrange("p (t c) -> p t c", c=NIX)
            idv = ids_of("lora0").rearrange("p (t b) -> p t b", b=BA)
            dve.tensor_scalar(ix[:, :, 0:BA], idv, float(P), const("col"), ALU.mult, ALU.add).then_inc(t_step, 1)
            dve.tensor_scalar(ix[:, :, BA:NIX], ids_of("lora0_own").rearrange("p (t o) -> p t o", o=1),
                              float(RANK), const("mod16"), ALU.mult, ALU.add).then_inc(t_step, 1)
            dve.wait_ge(t_step, 2)
            dve.tensor_copy(index, index_f).then_inc(index_ready, 1)

            steps = [0]

            def table(ins):
                steps[0] += 1
                ins.then_inc(table_step, 1)
                dve.wait_ge(table_step, steps[0])

            def make_tables():
                col = const("col")
                table(dve.tensor_copy(ids_f, ids))

                def idf(name):
                    return ids_f[:, IDS[name][0]:IDS[name][0] + IDS[name][1]]

                for n, name in enumerate(("sess_own", "cond_own")):
                    table(dve.tensor_scalar(row1_f[:, n * NG:(n + 1) * NG], idf(name), float(S), const("mod32"),
                                            ALU.mult, ALU.add))
                table(dve.tensor_copy(index1, row1_f))
                table(dve.tensor_scalar(clen, idf("len_own"), const("mod32"), WS, ALU.is_gt, ALU.mult))
                for k in range(KH):
                    table(dve.tensor_scalar(tmask[:, k, :], idf("seq"), const("hcol")[:, k:k + 1], None, ALU.is_gt))
                table(dve.tensor_scalar(onehot, idf("sess"), col, None, ALU.is_equal))
                dve.wait_ge(table_mm, 1)
                for half in range(2):
                    at = slice(half * HID, (half + 1) * HID)
                    table(dve.tensor_copy(bias_hid[at, :], bank[7][at, 0:B].rearrange("p (n t) -> p n t", t=2)[:, :, half]))
                table(dve.tensor_scalar(onehot, idf("adapter"), col, None, ALU.is_equal))
                table(dve.tensor_reduce(count[:, 0:1], onehot, AX_X, ALU.add))
                table(dve.tensor_scalar(count_i[:, 0:1], count[:, 0:1], float(GB - 1), None, ALU.add))
                table(dve.tensor_scalar(count_i[:, 1:2], count_i[:, 0:1], 2, 2, ALU.logical_shift_right,
                                        ALU.logical_shift_left))
                table(dve.tensor_copy(count[:, 1:2], count_i[:, 1:2]))
                table(dve.tensor_scalar(spread, const("ones"), count[:, 1:2], None, ALU.mult))
                table(dve.tensor_scalar(later, idf("adapter"), col, None, ALU.is_gt))
                table(dve.scalar_tensor_tensor(same, idf("adapter"), idf("adapter_own"), const("before"),
                                               ALU.is_equal, ALU.mult))
                dve.wait_ge(table_mm, 2)
                table(dve.tensor_copy(place, bank[6][:, 0:B]))
                for j in range(NCH):
                    slot = const("slot")[:, j:j + 1]
                    dve.scalar_tensor_tensor(junk[0], place, slot, const("batch1"), ALU.is_equal, ALU.mult,
                                             accum_out=at_place[:, j:j + 1])
                    table(dve.scalar_tensor_tensor(junk[1], place, slot, idf("adapter"), ALU.is_equal, ALU.mult,
                                                   accum_out=at_adapter[:, j:j + 1]))
                table(dve.tensor_copy(adapter, at_adapter))
                table(dve.tensor_scalar(row_f, at_place, -1.0, 0.0, ALU.add, ALU.max))
                table(dve.tensor_scalar(row_f, row_f, float(S), const("mod32"), ALU.mult, ALU.add))
                table(dve.tensor_copy(rows_in, row_f))
                table(dve.tensor_scalar(empty, at_place, 0.5, float(NO_ROW), ALU.is_lt, ALU.mult))
                table(dve.tensor_tensor(row_f, row_f, empty, ALU.add))
                table(dve.tensor_copy(rows_out, row_f))

            for n, (_, w, hi, lo, stores) in enumerate(jobs):
                if n == tables:
                    make_tables()
                dve.wait_ge(prep_hi, n + 1)
                if stores and n >= RING:
                    dve.wait_ge(table_stored[n % RING], 32 * (n // RING))
                dve.scalar_tensor_tensor(lo, prep_in[n % RING][:, 0:w], WS, hi, ALU.mult, ALU.subtract).then_inc(prep_lo, 1)

            def t_parts(i, kind, src):
                dve.wait_ge(t_ready, i * 3 + kind + 1)
                dve.scalar_tensor_tensor(tf, src, 0.5 * IWS, own_batch, ALU.mult, ALU.mult).then_inc(t_step, 1)
                dve.wait_ge(t_step, i * 6 + 2 * kind + 1 + 2)
                dve.tensor_copy(t_part[kind][0], tf).then_inc(t_step, 1)
                dve.wait_ge(t_step, i * 6 + 2 * kind + 2 + 2)
                dve.tensor_tensor(t_part[kind][1], tf, t_part[kind][0], ALU.subtract).then_inc(t_split, 1)
                dve.wait_ge(t_split, i * 3 + kind + 1)

            def act_parts(i, f, p):
                q = (p + f) % 2
                dve.wait_ge(up_ready, i * NF + f + 1)
                dve.wait_ge(silu_done, i * NF + f + 1)
                dve.scalar_tensor_tensor(prod[q], bank[2 + q][:, 0:TA], IWS, sil[q], ALU.mult, ALU.mult).then_inc(prod_done, 1)
                dve.wait_ge(prod_done, i * NF + f + 1 + CR_PROD)
                dve.tensor_copy(act[0][:, f, :], prod[q]).then_inc(act_hi, 1)
                dve.wait_ge(act_hi, i * NF + f + 1)
                dve.tensor_tensor(act[1][:, f, :], prod[q], act[0][:, f, :], ALU.subtract).then_inc(act_split, 1)

            with dve.Fori(0, NA // 2) as it:
                for p in range(2):
                    i = it * 2 + p
                    t_parts(i, 0, bank[4][:, 0:TA])
                    t_parts(i, 1, bank[5][:, 0:TA])
                    for f in range(NF):
                        act_parts(i, f, p)
                        if f == 1:
                            dve.wait_ge(dq_loaded, (i + 1) * 48)
                            dve.tensor_scalar(dq_q, dq_q, shift[:, 0:1], 15, ALU.logical_shift_right,
                                              ALU.bitwise_and)
                        if 2 <= f < 10:
                            j = f - 2
                            ins = dve.tensor_scalar(dq_z.rearrange("p (n j) -> p n j", j=8)[:, :, j], dq_zp,
                                                    4 * j, 15, ALU.logical_shift_right, ALU.bitwise_and)
                            if j == 7:
                                ins.then_inc(dq_bits, 1)
                    dve.wait_ge(dq_bits, i * 2 + 1)
                    dve.tensor_tensor(dq_n, dq_q, dq_z, ALU.subtract).then_inc(dq_bits, 1)
                    t_parts(i, 2, bank[4][:, 0:TA])
                    dve.wait_ge(c0_stored, i * 32 + 32)
                    for hc in range(KH):
                        dve.wait_ge(down_ready, i * 4 + hc + 1 + CR_DOWN)
                        src = bank[6 + hc % 2][:, 0:TA]
                        dve.tensor_scalar(c0_part[0][:, hc, :], src, IWS, None, ALU.mult).then_inc(c0_hi, 1)
                        dve.wait_ge(c0_hi, i * 4 + hc + 1)
                        dve.scalar_tensor_tensor(c0_part[1][:, hc, :], src, IWS, c0_part[0][:, hc, :],
                                                 ALU.mult, ALU.subtract).then_inc(c0_split, 1)
            def deq2(i):
                def step(ins, n):
                    ins.then_inc(deq2_step, 1)
                    dve.wait_ge(deq2_step, i * 6 + n)

                here = bass.ds(i * DQ2, DQ2)
                dve.wait_ge(deq2_loaded, i * 48 + 48)
                step(dve.tensor_scalar(p2_in, p2_in, shift[:, 1:2], 15, ALU.logical_shift_right, ALU.bitwise_and), 1)
                step(dve.tensor_scalar(n2, p2_in, -8.0, WS, ALU.add, ALU.mult), 2)
                step(dve.tensor_scalar(e2, m2_in, 0.5, 0.5, ALU.mult, ALU.add), 3)
                step(dve.tensor_tensor(e2, e2, s2_in, ALU.mult), 4)
                step(dve.tensor_tensor(n2, n2, e2, ALU.mult), 5)
                step(dve.tensor_copy(w2_part[0][:, here], n2), 6)
                dve.tensor_tensor(w2_part[1][:, here], n2, w2_part[0][:, here], ALU.subtract).then_inc(deq2_done, 1)
                dve.wait_ge(deq2_done, i + 2)

            with dve.Fori(0, NB // 2) as it:
                for p in range(2):
                    i = it * 2 + p
                    for f in range(NF):
                        q = (p + f) % 2
                        n = i * NF + f
                        dve.wait_ge(up2_ready, n + 1)
                        dve.wait_ge(silu2_done, n + 1)
                        dve.scalar_tensor_tensor(prod2[q], bank[2 + q][:, :], IWS, sil2[q], ALU.mult,
                                                 ALU.mult).then_inc(prod2_done, 1)
                        dve.wait_ge(prod2_done, n + 1 + CR_PROD)
                        dve.tensor_copy(act2[0][:, f, :], prod2[q]).then_inc(act2_hi, 1)
                        dve.wait_ge(act2_hi, n + 1)
                        dve.tensor_tensor(act2[1][:, f, :], prod2[q], act2[0][:, f, :], ALU.subtract
                                          ).then_inc(act2_split, 1)
                        if f == 4:
                            dve.wait_ge(late_hi, i + 1)
                            dve.scalar_tensor_tensor(late_part[1], late_in, WS, late_part[0], ALU.mult,
                                                     ALU.subtract).then_inc(late_split, 1)
                        if f == 6:
                            deq2(i)

            def step_b(i, u):
                g, v = i - 1, (u - 1) % 4
                if valid(g, 0, NG):
                    dve.wait_ge(c2_hi, g + 1)
                    dve.scalar_tensor_tensor(c2[v % 2][1], bank[6][:, :], IWS, c2[v % 2][0], ALU.mult, ALU.subtract
                                             ).then_inc(c2_split, 1)
                g, v = i, u
                if valid(g, 0, NG):
                    def step(ins, n):
                        ins.then_inc(r_step, 1)
                        dve.wait_ge(r_step, g * 8 + n)
                        if n in (1, 2):
                            dve.sem_inc(dve_turns, 1)

                    dve.wait_ge(router_ready, g + 1)
                    step(dve.tensor_scalar(lg, bank[4][:, EXP * R1:WAR], IWS, None, ALU.mult), 1)
                    step(dve.max(mx8, lg), 2)
                    step(dve.max_index(ix8, mx8, lg), 3)
                    dve.tensor_tensor(gap[:, 0:1], mx8[:, 0:1], mx8[:, 1:2], ALU.subtract).then_inc(gap_ready, 1)
                    step(dve.tensor_copy(ixf[:, 0:2], ix8[:, 0:2]), 4)
                    dve.wait_ge(tanh_done, g + 1)
                    step(dve.scalar_tensor_tensor(pp[:, 0:2], const("sign"), th[:, 0:1], const("one"), ALU.mult,
                                                  ALU.add), 5)
                    for n in range(2):
                        step(dve.tensor_scalar(e1x[n], const("iota8"), ixf[:, n:n + 1], pp[:, n:n + 1], ALU.is_equal,
                                               ALU.mult), 6 + n)
                    step(dve.tensor_tensor(e1x[2], e1x[0], e1x[1], ALU.add), 8)
                    if valid(g - 1, 0, NG):
                        dve.wait_ge(hwt_ready, g)
                    dve.scalar_tensor_tensor(
                        hw.rearrange("p (e r) -> p e r", e=EXP), bank[4][:, 0:EXP * R1].rearrange("p (e r) -> p e r", e=EXP),
                        IWS, e1x[2].rearrange("p (e o) -> p e o", o=1).broadcast_to((P, EXP, R1)), ALU.mult, ALU.mult
                    ).then_inc(hw_done, 1)
                g, v = i + 1, (u + 1) % 4
                if valid(g, 0, NG):
                    dve.wait_ge(mixed_ready, g + 1)
                    c1v = c1_f.rearrange("p (n s) -> p n s", s=S)
                    dve.scalar_tensor_tensor(
                        c1v, bank[2][:, :].rearrange("p (n s) -> p n s", s=S), IWS,
                        bias_of("mix1").rearrange("p (o s) -> p o s", o=1).broadcast_to((P, KH * GB, S)),
                        ALU.mult, ALU.add).then_inc(c1_step, 1)
                    dve.wait_ge(c1_step, g * 3 + 1)
                    c1m = c1_f.rearrange("p (k b s) -> p k b s", k=KH, b=GB)
                    dve.tensor_tensor(c1m, c1m, tmask[:, :, bass.ds(g * GB, GB)].rearrange(
                        "p k (b o) -> p k b o", o=1).broadcast_to((P, KH, GB, S)), ALU.mult).then_inc(c1_step, 1)
                    dve.wait_ge(c1_step, g * 3 + 2)
                    dve.tensor_copy(c1[v % 2][0], c1_f).then_inc(c1_step, 1)
                    dve.wait_ge(c1_step, g * 3 + 3)
                    dve.tensor_tensor(c1[v % 2][1], c1_f, c1[v % 2][0], ALU.subtract).then_inc(c1_split, 1)
                g, v = i - 1, (u - 1) % 4
                if valid(g, 0, NG):
                    dve.wait_ge(y3_ready, g + 1)
                    dve.wait_ge(x2b_done, g + 1)
                    if valid(g - 2, 0, NG):
                        dve.wait_ge(x3_stored[v % 2], slot_count(g - 2, v, 2))
                    dve.scalar_tensor_tensor(x3_f[v % 2], bank[7][:, :], IWS, x2b[v % 2], ALU.mult, ALU.add
                                             ).then_inc(x3_done, 1)
                g, v = i, u
                if valid(g, 0, NG):
                    dve.wait_ge(hwt_ready, g + 1)
                    dve.tensor_copy(hwt[0], bank[5][:, 0:P]).then_inc(hwt_hi, 1)
                    dve.wait_ge(hwt_hi, g + 1)
                    dve.tensor_tensor(hwt[1], bank[5][:, 0:P], hwt[0], ALU.subtract).then_inc(hwt_split, 1)
                g, v = i + 2, (u + 2) % 4
                if valid(g, 0, NG):
                    for pair in range(2):
                        dve.wait_ge(hid_hi, 2 * g + pair + 1)
                        dve.tensor_tensor(hid[v % 2][pair][1], hid_f[pair], hid[v % 2][pair][0], ALU.subtract
                                          ).then_inc(hid_split, 1)
                g, v = i, u
                if valid(g, 0, NG):
                    dve.wait_ge(x2_ready, g + 1)
                    dve.wait_ge(x1b_done, g + 1)
                    if valid(g - 2, 0, NG):
                        dve.wait_ge(x2b_done, g - 1)
                    dve.scalar_tensor_tensor(x2_f[v % 2], bank[3][:, :], IWS, x1b[v], ALU.mult, ALU.add
                                             ).then_inc(x2_done, 1)

            run_b(dve, step_b)
            dve.wait_ge(x2b_done, NG)
            for s in x3_stored:
                dve.wait_ge(s, 16 * NG // 2)
            dve.memset(sc8, -3.0e38)
            dve.memset(hl, 0.0).then_inc(g_step, 1)
            dve.wait_ge(g_step, 1)

            def step_c(i, u):
                j, v = i, u
                if valid(j, 0, NCH):
                    def step(ins, n):
                        ins.then_inc(g_step, 1)
                        dve.wait_ge(g_step, j * 8 + n + 1)
                        if n in (1, 2):
                            dve.sem_inc(dve_turns, 1)

                    dve.wait_ge(ag3_ready, 2 * j + 1)
                    step(dve.scalar_tensor_tensor(sc8[:, 0:NR3], bank[4][:, R3:WAG], IWS, bias_of("gate3"), ALU.mult,
                                                  ALU.add), 1)
                    step(dve.max(mc8, sc8), 2)
                    dve.tensor_scalar(negm[:, 0:1], mc8[:, 0:1], -1.0, None, ALU.mult).then_inc(negm_ready, 1)
                    step(dve.max_index(ic8, mc8, sc8), 3)
                    step(dve.tensor_copy(icf[:, 0:1], ic8[:, 0:1]), 4)
                    dve.wait_ge(exp_done, j + 1)
                    step(dve.reciprocal(rec[:, 0:1], esum[:, 0:1]), 5)
                    step(dve.reciprocal(wn[:, 1:2], rec[:, 0:1]), 6)
                    step(dve.tensor_tensor(wn[:, 0:1], rec[:, 0:1], wn[:, 1:2], ALU.mult), 7)
                    step(dve.tensor_scalar(keep, const("level"), icf[:, 0:1], wn[:, 0:1], ALU.is_le, ALU.mult), 8)
                    if valid(j - 1, 0, NCH):
                        dve.wait_ge(hlt_ready, j)
                    dve.scalar_tensor_tensor(hl[:, 0:R3], bank[4][:, 0:R3], IWS, keep, ALU.mult, ALU.mult
                                             ).then_inc(hl_done, 1)
                j, v = i + 1, (u + 1) % 4
                if valid(j, 0, NCH):
                    dve.wait_ge(ct3_hi, j + 1)
                    dve.tensor_tensor(c3t[v % 2][1], bank[2][:, :], c3t[v % 2][0], ALU.subtract).then_inc(ct3_split, 1)
                j, v = i, u
                if valid(j, 0, NCH):
                    dve.wait_ge(hlt_ready, j + 1)
                    dve.tensor_copy(hlt[0], bank[5][:, 0:P]).then_inc(hlt_hi, 1)
                    dve.wait_ge(hlt_hi, j + 1)
                    dve.tensor_tensor(hlt[1], bank[5][:, 0:P], hlt[0], ALU.subtract).then_inc(hlt_split, 1)
                j, v = i + 3, (u + 3) % 4
                if valid(j, 0, NCH):
                    dve.wait_ge(xt3_hi, j + 1)
                    dve.tensor_tensor(x3t[v % 2][1], bank[0][:, :], x3t[v % 2][0], ALU.subtract).then_inc(xt3_split, 1)
                j, v = i, u
                if valid(j, 0, NCH):
                    dve.wait_ge(fin_ready, j + 1)
                    dve.wait_ge(x3b_done, j + 1)
                    if valid(j - 2, 0, NCH):
                        dve.wait_ge(fin_stored[v % 2], slot_count(j - 2, v, 2))
                    dve.scalar_tensor_tensor(fin[v % 2], bank[3][:, :], IWS, x3b[v], ALU.mult, ALU.add
                                             ).then_inc(fin_done, 1)

            run_c(dve, step_c)

        @block.tensor
        def _(pe):
            pe.sem_inc(down_ready, CR_DOWN)
            pe.wait_ge(const_in, 80)
            pe.wait_ge(table_step, 10)
            pe.matmul(bank[7][:, 0:B], b_sess, onehot, start=True, stop=True).then_inc(table_mm, 1)
            pe.wait_ge(table_step, 20)
            pe.matmul(bank[6][:, 0:B], spread, later, start=True, stop=False)
            pe.matmul(bank[6][:, 0:B], const("ones"), same, start=False, stop=True).then_inc(table_mm, 1)
            with pe.Fori(0, NA // 2) as it:
                for p in range(2):
                    i = it * 2 + p
                    lav = la[p].rearrange("p (h c m) -> p h c m", h=2, m=P)
                    xv = [xt[p][h].rearrange("p (k t) -> p k t", k=KH) for h in range(2)]
                    pe.wait_ge(la_ready, i + 1)
                    pe.wait_ge(lb_loaded[p], (it + 1) * 16)
                    pe.wait_ge(x_split, i + 2)
                    for kind in range(2):
                        for k in range(KH):
                            c = kind * KH + k
                            last = mm3(pe, bank[4 + kind][:, 0:TA],
                                       [lav[:, h, c, :] for h in range(2)],
                                       [xv[h][:, k, :] for h in range(2)], k == 0, k == KH - 1)
                        last.then_inc(t_ready, 1)
                    for f in range(NF):
                        q = (p + f) % 2
                        pe.wait_ge(prep_lo, jobs_for((f + 1) * chunk))
                        pe.wait_ge(prod_done, i * NF + f + 1)
                        for g in range(2):
                            o = bank[2 * g + q][:, 0:TA]
                            for k in range(KH):
                                mm3(pe, o, [wgu[h][:, f, g, k, :] for h in range(2)],
                                    [xv[h][:, k, :] for h in range(2)], k == 0, False)
                            if f == 0:
                                pe.wait_ge(t_split, i * 3 + g + 1)
                            at = (g * NF + f) * P
                            mm3(pe, o, [lb[p][:, h * LB + at:h * LB + at + P] for h in range(2)],
                                t_part[g], False, True).then_inc([gate_ready, up_ready][g], 1)
                    for f in range(NF):
                        pe.wait_ge(act_split, i * NF + f + 1)
                        last = mm3(pe, bank[4][:, 0:TA], [lav[:, h, 2 * KH + f, :] for h in range(2)],
                                   [act[h][:, f, :] for h in range(2)], f == 0, f == NF - 1)
                    last.then_inc(t_ready, 1)
                    pe.wait_ge(prep_lo, len(jobs))
                    for hc in range(KH):
                        o = bank[6 + hc % 2][:, 0:TA]
                        pe.wait_ge(c0_split, i * 4 + hc + 1)
                        for f in range(NF):
                            mm3(pe, o, [wdn[h][:, f, hc * P:(hc + 1) * P] for h in range(2)],
                                [act[h][:, f, :] for h in range(2)], f == 0, False)
                        if hc == 0:
                            pe.wait_ge(t_split, i * 3 + 3)
                        at = 2 * FP + hc * P
                        mm3(pe, o, [lb[p][:, h * LB + at:h * LB + at + P] for h in range(2)],
                            t_part[2], False, True).then_inc(down_ready, 1)
            pe.wait_ge(c0_split, 4 * NA + CR_C0)
            with pe.Fori(0, NB // 2) as it:
                for p in range(2):
                    i = it * 2 + p
                    pe.wait_ge(ct_loaded[p], (it + 1) * 32)
                    for f in range(NF):
                        q = (p + f) % 2
                        pe.wait_ge(wq_loaded[f], 32)
                        pe.wait_ge(prod2_done, i * NF + f + 1)
                        for g in range(2):
                            o = bank[2 * g + q][:, :]
                            for k in range(KH):
                                last = mm3(pe, o, [wgu[h][:, f, g, k, :] for h in range(2)],
                                           [ct[p][h][:, k, :] for h in range(2)], k == 0, k == KH - 1)
                            last.then_inc([gate2_ready, up2_ready][g], 1)
                    pe.wait_ge(wq_loaded[NF], 32)
                    for g in range(4):
                        pe.wait_ge(out16_done, i * 4 + 4)
                        for f in range(NF):
                            if g == 0:
                                pe.wait_ge(act2_split, i * NF + f + 1)
                            last = mm3(pe, bank[4 + g][:, :], [act2[h][:, f, g * P:(g + 1) * P] for h in range(2)],
                                       [wdn[h][:, f, :] for h in range(2)], f == 0, f == NF - 1)
                        last.then_inc(down2_ready, 1)
            pe.wait_ge(out16_done, 4 * NB + 4)
            pe.wait_ge(prod2_done, NF * NB + CR_PROD)
            pe.wait_ge(wb_loaded, 32)
            pe.wait_ge(deq2_done, NB + 1)

            def step_b(i, u):
                g, v = i, u
                if valid(g, 0, NG):
                    pe.wait_ge(c1_split, g + 1)
                    if valid(g - 1, 0, NG):
                        pe.wait_ge(hw_done, g)
                        pe.wait_ge(x2_done, g)
                    cv = [w.rearrange("p (k t) -> p k t", k=KH) for w in c1[v % 2]]
                    for k in range(KH):
                        last = mm3(pe, bank[4][:, 0:WAR], [w[:, k, :] for w in cv], [w[:, k, :] for w in w_ar1],
                                   k == 0, k == KH - 1)
                    last.then_inc(router_ready, 1)
                    for k in range(KH):
                        mm3(pe, bank[3][:, :], [w[:, k, :] for w in cv], [w[:, k, :] for w in w_base1], k == 0, False)
                g, v = i - 1, (u - 1) % 4
                if valid(g, 0, NG):
                    pe.wait_ge(x2_split, g + 1)
                    pe.wait_ge(bd2_ready, g + 1)
                    if valid(g - 1, 0, NG):
                        pe.wait_ge(c2_split, g)
                    for k in range(KH):
                        last = mm3(pe, bank[6][:, k * P:(k + 1) * P], [w[:, k * P:(k + 1) * P] for w in x2_part[v % 2]],
                                   bd2[v % 2], True, True)
                    last.then_inc(c2_ready, 1)
                g, v = i + 1, (u + 1) % 4
                if valid(g, 0, NG):
                    pe.wait_ge(hid_split, 2 * g + 2)
                    if valid(g - 1, 0, NG):
                        pe.wait_ge(c1_step, 3 * g)
                    for k in range(KH):
                        for pair in range(2):
                            at = k * P + pair * 2 * S
                            last = mm3(pe, bank[2][:, at:at + 2 * S],
                                       [w[:, k * P:(k + 1) * P] for w in hid[v % 2][pair]],
                                       [w[:, 0, :] for w in w_mix1], True, True)
                    last.then_inc(mixed_ready, 1)
                g, v = i - 1, (u - 1) % 4
                if valid(g, 0, NG):
                    pe.wait_ge(c2_split, g + 1)
                    if valid(g - 1, 0, NG):
                        pe.wait_ge(x3_done, g)
                    for k in range(KH):
                        last = mm3(pe, bank[7][:, :], [w[:, k * P:(k + 1) * P] for w in c2[v % 2]],
                                   [w[:, k, :] for w in w_2], k == 0, k == KH - 1)
                    last.then_inc(y3_ready, 1)
                g, v = i, u
                if valid(g, 0, NG):
                    pe.wait_ge(hw_done, g + 1)
                    if valid(g - 1, 0, NG):
                        pe.wait_ge(hwt_split, g)
                    pe.transpose(bank[5][:, 0:P], hw, const("ident")).then_inc(hwt_ready, 1)
                g, v = i + 2, (u + 2) % 4
                if valid(g, 0, NG):
                    pe.wait_ge(x1_split, g + 1)
                    pe.wait_ge(bd1_ready, g + 1)
                    if valid(g - 1, 0, NG):
                        pe.wait_ge(gelu_done, 2 * g)
                    for pair in range(2):
                        mm3(pe, bank[pair][:, :], [w[:, pair * P:(pair + 1) * P] for w in bd1[v % 2]],
                            x1_part[v % 2], True, True).then_inc(hid_ready, 1)
                g, v = i, u
                if valid(g, 0, NG):
                    pe.wait_ge(hwt_split, g + 1)
                    mm3(pe, bank[3][:, :], hwt, [w[:, 0, :] for w in w_b1], False, True).then_inc(x2_ready, 1)

            run_b(pe, step_b)
            pe.wait_ge(wc_loaded, 32)
            pe.wait_ge(w3_loaded, 32)
            pe.wait_ge(x3_done, NG)

            def step_c(i, u):
                j, v = i, u
                if valid(j, 0, NCH):
                    pe.wait_ge(ct3_split, j + 1)
                    if valid(j - 1, 0, NCH):
                        pe.wait_ge(hl_done, j)
                        pe.wait_ge(fin_done, j)
                    for k in range(KH):
                        last = mm3(pe, bank[4][:, 0:WAG], [w[:, k * P:(k + 1) * P] for w in c3t[v % 2]],
                                   [w[:, k, :] for w in w_ag3], k == 0, k == KH - 1)
                    last.then_inc(ag3_ready, 1)
                    for k in range(KH):
                        last = mm3(pe, bank[3][:, :], [w[:, k * P:(k + 1) * P] for w in c3t[v % 2]],
                                   [w[:, k, :] for w in w_base3], k == 0, False)
                    last.then_inc(ag3_ready, 1)
                j, v = i + 1, (u + 1) % 4
                if valid(j, 0, NCH):
                    pe.wait_ge(c3_done, j + 1)
                    if valid(j - 1, 0, NCH):
                        pe.wait_ge(ct3_split, j)
                    for k in range(KH):
                        last = pe.transpose(bank[2][:, k * P:(k + 1) * P], c3_f[v % 2][:, k * P:(k + 1) * P],
                                            const("ident"))
                    last.then_inc(ct3_ready, 1)
                j, v = i + 2, (u + 2) % 4
                if valid(j, 0, NCH):
                    pe.wait_ge(xt3_split, j + 1)
                    if valid(j - 1, 0, NCH):
                        pe.wait_ge(c3_done, j)
                    which = pe.value_load(adapter[0:1, bass.ds(j, 1)], min_val=0, max_val=AD3 - 1)
                    for k in range(KH):
                        last = mm3(pe, bank[1][:, :].rearrange("p (o c) -> p o c", o=1),
                                   [w[:, k * P:(k + 1) * P] for w in x3t[v % 2]],
                                   [w[:, bass.ds(which, 1), k, :] for w in w3], k == 0, k == KH - 1)
                    last.then_inc(cond3_ready, 1)
                j, v = i, u
                if valid(j, 0, NCH):
                    pe.wait_ge(hl_done, j + 1)
                    if valid(j - 1, 0, NCH):
                        pe.wait_ge(hlt_split, j)
                    pe.transpose(bank[5][:, 0:P], hl, const("ident")).then_inc(hlt_ready, 1)
                j, v = i + 3, (u + 3) % 4
                if valid(j, 0, NCH):
                    pe.wait_ge(x3_loaded[v], slot_count(j, v, 4))
                    if valid(j - 1, 0, NCH):
                        pe.wait_ge(xt3_split, j)
                    for k in range(KH):
                        last = pe.transpose(bank[0][:, k * P:(k + 1) * P], x3_in[v][:, k * P:(k + 1) * P],
                                            const("ident"))
                    last.then_inc(xt3_ready, 1)
                j, v = i, u
                if valid(j, 0, NCH):
                    pe.wait_ge(hlt_split, j + 1)
                    mm3(pe, bank[3][:, :], hlt, [w[:, 0, :] for w in w_b3], False, True).then_inc(fin_ready, 1)

            run_c(pe, step_c)


def block_layout(gate, up, down, fill):
    gu = np.full((2, H, FP), fill, gate.dtype)
    gu[0, :, :FF], gu[1, :, :FF] = gate, up
    dn = np.full((FP, H), fill, down.dtype)
    dn[:FF] = down
    gu = gu.reshape(2, KH, P, NF, P).transpose(2, 3, 0, 1, 4).reshape(P, GU)
    dn = dn.reshape(NF, P, H).transpose(1, 0, 2).reshape(P, DN)
    return np.ascontiguousarray(np.concatenate([gu, dn], axis=1))


def row_layout(gate, up, down):
    n = FP * gate.shape[1] // FF
    gu = np.zeros((2, KH, n), gate.dtype)
    gu[0, :, :gate.shape[1]], gu[1, :, :up.shape[1]] = gate, up
    gu = gu.reshape(2, KH, NF, n // NF).transpose(2, 0, 1, 3).reshape(-1)
    return np.ascontiguousarray(np.concatenate([gu, down.reshape(-1)]).reshape(1, -1))


def arrays(i):
    i = {k: np.asarray(v) for k, v in i.items()}
    d = {}
    x = i["x"].reshape(TOK, H)
    d["x"] = x
    d["xt"] = np.ascontiguousarray(x.T)
    d["w_cond"] = block_layout(i["L0_cond_W_gate"].T, i["L0_cond_W_up"].T, i["L0_cond_W_down"].T, 0)
    a = [i[f"L0_cond_A_{n}"][0] for n in ("gate", "up")]
    ad = np.zeros((ADAPT, RANK, FP), np.float32)
    ad[:, :, :FF] = i["L0_cond_A_down"][0]
    parts = [v.reshape(ADAPT, RANK, -1, P).transpose(0, 3, 2, 1).reshape(ADAPT * P, -1) for v in (*a, ad)]
    d["lora_a"] = np.ascontiguousarray(np.concatenate(parts, axis=1))
    bs = []
    for n in ("gate", "up"):
        b = np.zeros((ADAPT, RANK, FP), np.float32)
        b[:, :, :FF] = i[f"L0_cond_B_{n}"][0].transpose(0, 2, 1)
        bs.append(b.reshape(ADAPT * RANK, FP))
    bs.append(i["L0_cond_B_down"][0].transpose(0, 2, 1).reshape(ADAPT * RANK, H))
    d["lora_b"] = np.ascontiguousarray(np.concatenate(bs, axis=1))
    d["q"] = block_layout(*(np.repeat(i[f"L0_ffn_{n}_qweight"], 8, axis=0) for n in ("gate", "up", "down")), 0)
    d["z"] = row_layout(*(i[f"L0_ffn_{n}_zeros"] for n in ("gate", "up", "down")))
    d["s"] = row_layout(*(i[f"L0_ffn_{n}_scales"] for n in ("gate", "up", "down")))
    p = np.arange(P)
    b = np.arange(B)
    level = np.searchsorted([8, 16, 32], np.arange(R3), side="right")
    d["consts"] = np.concatenate([np.broadcast_to(v, (P, CONSTS[n][1])) for n, v in {
        "col": p[:, None], "mod16": p[:, None] % RANK, "mod32": p[:, None] % S,
        "hcol": p[:, None] + P * np.arange(KH), "iota8": np.arange(8), "sign": [1, -1], "one": [1, 1],
        "level": level, "blocks": p[:, None] // S == np.arange(GB), "batch1": b + 1, "before": p[:, None] < b,
        "slot": p[:, None] // S + GB * np.arange(NCH), "ones": np.ones(P), "ident": np.eye(P),
        "own_batch": p[:, None] // RANK == np.arange(TA) // S}.items()], axis=1).astype(np.float32)
    d["shift"] = np.concatenate([(p % 8 * 4)[:, None], np.repeat((p % 2 * 4)[:, None], 7, axis=1)], axis=1).astype(np.int32)
    a0, sess, seq, cond, a3, lens = (i[n] for n in (
        "itok_B_2_6", "itok_B_0_7", "itok_B_2182_4065", "itok_B_0_15", "itok_B_3_7", "_lenS"))

    def own(v, rows):
        return np.repeat(v.reshape(-1, P // rows), rows, axis=1).T

    d["ids"] = np.ascontiguousarray(np.concatenate([np.broadcast_to(v, (P, IDS[n][1])) for n, v in {
        "lora0": a0, "lora0_own": own(a0, RANK), "sess_own": own(sess, S), "cond_own": own(cond, S),
        "len_own": own(lens, S), "sess": sess, "seq": seq, "adapter": a3, "adapter_own": a3[:, None]}.items()], axis=1))
    d["biases"] = np.ascontiguousarray(np.broadcast_to(np.concatenate(
        [i[n] for n in ("L1_cond_b2", "L1_ffn_b_base", "L2_ffn_bias", "L3_ffn_b", "L3_ffn_gate_b")]), (P, NBIAS)))
    bs = np.zeros((P, P), np.float32)
    bs[:NSESS, :HID] = bs[:NSESS, HID:] = i["L1_cond_b_sess"]
    d["b_sess"] = bs
    d["w_sess"] = i["L1_cond_W_sess"].reshape(NSESS * S, HID)
    d["w_mix2"] = i["L2_cond_weights"].reshape(NCOND * S, S)

    def k_tiles(w):
        return w.reshape(KH, P, -1).transpose(1, 0, 2).reshape(P, -1)

    mix = np.zeros((2, HID, 2, S), np.float32)
    mix[0, :, 0], mix[1, :, 1] = i["L1_cond_W2"], i["L1_cond_W2"]
    b3 = np.zeros((P, H), np.float32)
    b3[:R3] = i["L3_ffn_B"].T
    d["late"] = np.ascontiguousarray(np.concatenate([
        k_tiles(i["L1_ffn_W_base"].T),
        k_tiles(np.concatenate([i["L1_ffn_A"].reshape(EXP * R1, H), i["L1_ffn_W_router"]]).T),
        i["L1_ffn_B"].transpose(0, 2, 1).reshape(P, H), mix.reshape(P, 2 * S),
        k_tiles(i["L3_ffn_W"].T), k_tiles(np.concatenate([i["L3_ffn_A"], i["L3_ffn_gate_w"]]).T), b3,
        *(k_tiles(w.T) for w in i["L3_cond_weight"])], axis=1))
    d["p2"] = np.ascontiguousarray(k_tiles(np.repeat(i["L2_ffn_weight_packed"].reshape(H, H // 2).T, 2, axis=0)))
    d["s2"] = np.ascontiguousarray(k_tiles(np.repeat(i["L2_ffn_weight_scale"].reshape(H, H // 32).T, 32, axis=0)))
    d["m2"] = np.ascontiguousarray(k_tiles(np.repeat(
        i["L2_ffn_weight_var_mask"].reshape(H, H // 32).T, 32, axis=0)))
    return d


def kernel(**inputs):
    import concourse.bacc as bacc
    from concourse.bass_utils import run_bass_kernel_spmd

    nc = bacc.Bacc("TRN2", target_bir_lowering=False, num_devices=1)
    ins = arrays(inputs)
    d = {n: nc.dram_tensor(n + "_in", a.shape, mybir.dt.from_np(a.dtype), kind="ExternalInput").ap()
         for n, a in ins.items()}
    out = nc.dram_tensor("out", (TOK, H), F32, kind="ExternalOutput").ap()
    program(nc, d, out)
    got = run_bass_kernel_spmd(nc, [{n + "_in": a for n, a in ins.items()}], core_ids=[0])
    return got.results[0]["out"].reshape(B, S, H)
```

```python
import numpy as np
from contextlib import ExitStack

import concourse.bass as bass
from concourse import mybir

ALU = mybir.AluOpType
ACT = mybir.ActivationFunctionType
AX_X = mybir.AxisListType.X
F32 = mybir.dt.float32
F16 = mybir.dt.float16
I32 = mybir.dt.int32
U32 = mybir.dt.uint32
U8 = mybir.dt.uint8

P = 128
B, S, H = 128, 32, 512
TOK = B * S
KH = H // P
FF = 1376
NF = -(-FF // P)
FP = NF * P
RANK, ADAPT = 16, 16

WS = 256.0
IWS = 1.0 / WS

GU = NF * 2 * KH * P
DN = NF * H
WFLAT = GU + DN

TA = 256
NA = TOK // TA
BA = TA // S
assert BA * RANK == P
LA = (2 * KH + NF) * RANK
LB = 2 * FP + H
NIX = BA + 1
DQ = WFLAT // NA
assert DQ * NA == WFLAT and DQ % 8 == 0

TB = 512
NB = TOK // TB


GB = 4
NG = B // GB
HID = 64
NSESS, NCOND = 8, 16
EXP, R1 = 8, 16
WAR = EXP * R1 + EXP
AD3 = 8
NCH = (B + AD3 * (GB - 1)) // GB
R3, NR3 = 64, 4
WAG = R3 + NR3
NO_ROW = 2 * TOK

LATE_B = [("base1", KH * H), ("ar1", KH * WAR), ("b1", H), ("mix1", 2 * S)]
LATE_C = [("base3", KH * H), ("ag3", KH * WAG), ("b3", H)]
NLB, NLC = sum(n for _, n in LATE_B), sum(n for _, n in LATE_C)
NLW = AD3 * KH * H
NLATE = NLB + NLC + NLW
LQ = NLATE // NB
DQ2 = KH * H // NB
assert LQ * NB == NLATE

CONSTS = {}
for _name, _n in (("col", 1), ("mod16", 1), ("mod32", 1), ("hcol", KH), ("iota8", 8), ("sign", 2), ("one", 2),
                  ("level", R3), ("blocks", GB), ("number", B), ("before", B), ("places", NCH * GB), ("ones", NCH * GB),
                  ("ident", P), ("own_batch", TA)):
    CONSTS[_name] = (sum(n for _, n in CONSTS.values()), _n)
NCONST = sum(n for _, n in CONSTS.values())
BIASES = {}
for _name, _n in (("mix1", S), ("base1", H), ("ffn2", H), ("base3", H), ("gate3", NR3)):
    BIASES[_name] = (sum(n for _, n in BIASES.values()), _n)
NBIAS = sum(n for _, n in BIASES.values())
IDS = {}
for _name, _n in (("lora0", B), ("lora0_own", NA), ("sess_own", NG), ("cond_own", NG), ("len_own", NG),
                  ("sess", B), ("seq", B), ("adapter", B), ("adapter_own", 1)):
    IDS[_name] = (sum(n for _, n in IDS.values()), _n)
NIDS = sum(n for _, n in IDS.values())
NFIRST = B + NA


class Arena:

    def __init__(self, tensor):
        self.tensor, self.at, self.top = tensor, 0, 0

    def take(self, n, dtype):
        size = n * (2 if dtype == F16 else 4)
        start = self.at
        self.at += (size + 31) // 32 * 32
        self.top = max(self.top, self.at)
        ap = self.tensor[:, start // 2:(start + size) // 2]
        return ap if dtype == F16 else ap.bitcast(dtype)


def mm3(pe, out, a, b, start, stop):
    pe.matmul(out, a[0], b[0], start=start, stop=False)
    pe.matmul(out, a[0], b[1], start=False, stop=False)
    return pe.matmul(out, a[1], b[0], start=False, stop=stop)


def program(nc, d, out):
    ctx = ExitStack()
    with ctx:
        def psum(name):
            return ctx.enter_context(nc.psum_tensor(name, [P, 512], F32))

        def sem(name):
            return ctx.enter_context(nc.semaphore(name))

        room = Arena(ctx.enter_context(nc.sbuf_tensor("room", [P, 207 * 512], F16)))
        bank = [psum(f"bank{n}") for n in range(8)]

        def scratch(name, shape, dtype):
            return nc.dram_tensor(name, shape, dtype).ap()
        c0 = scratch("c0", (2, P, KH, TOK), F16)
        wq = scratch("wq", (2, P, WFLAT), F16)

        late = scratch("late", (2, P, NLATE), F16)
        x1 = scratch("x1", (TOK, H), F32)
        x3 = scratch("x3", (TOK, H), F32)

        w0 = [room.take(WFLAT, F16) for _ in range(2)]
        wgu = [w[:, 0:GU].rearrange("p (f g k c) -> p f g k c", f=NF, g=2, k=KH) for w in w0]
        wdn = [w[:, GU:WFLAT].rearrange("p (f c) -> p f c", f=NF) for w in w0]
        consts = room.take(NCONST, F32)
        biases = room.take(NBIAS, F32)
        ids = room.take(NIDS, I32)

        def const(name):
            return consts[:, CONSTS[name][0]:CONSTS[name][0] + CONSTS[name][1]]

        def bias_of(name):
            return biases[:, BIASES[name][0]:BIASES[name][0] + BIASES[name][1]]

        def ids_of(name):
            return ids[:, IDS[name][0]:IDS[name][0] + IDS[name][1]]

        own_batch = const("own_batch")
        shift = room.take(8, I32)
        index1 = room.take(2 * NG, I32)
        clen = room.take(NG, F32)
        tmask = room.take(KH * B, F32).rearrange("p (k b) -> p k b", k=KH)
        bias_hid = room.take(B // 2, F32)
        rows_in = room.take(NCH, I32)
        rows_out = room.take(NCH, I32)
        adapter = room.take(NCH, I32)
        index = room.take(NA * NIX, I32)
        index_f = room.take(NA * NIX, F32)
        stage_start = room.at

        la_0, prep_start, la_1 = room.take(BA * 2 * LA, F16), room.at, room.take(BA * 2 * LA, F16)
        lb_1, prep_end, lb_0 = room.take(2 * LB, F16), room.at, room.take(2 * LB, F16)
        la, lb = [la_0, la_1], [lb_0, lb_1]
        la_raw = room.take(BA * LA, F32)
        lb_raw = room.take(LB, F32)
        index_now = [room.take(NIX, I32) for _ in range(2)]
        xs = room.take(KH * TA, F32)
        xt = [[room.take(KH * TA, F16) for _ in range(2)] for _ in range(2)]
        tables_start = room.at
        act = [room.take(NF * TA, F16).rearrange("p (f t) -> p f t", f=NF) for _ in range(2)]
        sil = [room.take(TA, F32) for _ in range(2)]
        prod = [room.take(TA, F32) for _ in range(2)]
        tf = room.take(TA, F32)
        t_part = [[room.take(TA, F16) for _ in range(2)] for _ in range(3)]
        c0_part = [room.take(KH * TA, F16).rearrange("p (k t) -> p k t", k=KH) for _ in range(2)]
        tables_end = room.at
        dq_q = room.take(DQ, I32)
        dq_n = dq_q.bitcast(F32)
        dq_zp = room.take(DQ // 8, I32)
        dq_z = room.take(DQ, I32)
        dq_s = room.take(DQ, F16)
        dq_part = [room.take(DQ, F16) for _ in range(2)]
        table_room = Arena(room.tensor)
        table_room.at = tables_start
        b_sess = table_room.take(P, F32)
        ids_f = table_room.take(NIDS, F32)
        onehot = table_room.take(B, F32)
        later = table_room.take(B, F32)
        same = table_room.take(B, F32)
        count = table_room.take(4, F32)
        count_i = table_room.take(4, I32)
        spread = table_room.take(NCH * GB, F32)
        at_batch = table_room.take(NCH * GB, F32)
        own_adapter = table_room.take(P, F32)
        chosen = table_room.take(NCH * GB, F32)
        at_place = table_room.take(NCH, F32)
        row_f = table_room.take(NCH, F32)
        empty = table_room.take(NCH, F32)
        row1_f = table_room.take(2 * NG, F32)
        assert table_room.at <= tables_end
        PREP = 2 * KH * P
        RING = (prep_end - prep_start) // (4 * PREP)
        room.at = prep_start
        prep_in = [room.take(PREP, F32) for _ in range(RING)]
        assert room.at <= prep_end

        room.at = stage_start
        wb_part = [room.take(NLB, F16) for _ in range(2)]
        w2_part = [room.take(KH * H, F16) for _ in range(2)]
        mix1 = room.take(NG * HID, F32)
        mix2 = room.take(NG * S, F32)
        b_start = room.at
        late_in = room.take(LQ, F32)
        late_part = [room.take(LQ, F16) for _ in range(2)]
        p2_in = room.take(DQ2, I32)
        s2_in = room.take(DQ2, F16)
        m2_in = room.take(DQ2 // 2, F16).bitcast(U8)[:, 0:DQ2]
        n2 = room.take(DQ2, F32)
        e2 = room.take(DQ2, F32)
        ct = [[room.take(KH * TB, F16).rearrange("p (k t) -> p k t", k=KH) for _ in range(2)] for _ in range(2)]
        act2 = [room.take(NF * TB, F16).rearrange("p (f t) -> p f t", f=NF) for _ in range(2)]
        sil2 = [room.take(TB, F32) for _ in range(2)]
        prod2 = [room.take(TB, F32) for _ in range(2)]
        xn = [room.take(4 * H, F32).rearrange("p (g h) -> p g h", g=4) for _ in range(2)]
        out16 = [room.take(H, F16) for _ in range(2)]

        room.at = b_start
        wc_part = [room.take(NLC, F16) for _ in range(2)]
        c_start = room.at

        def ring(n, size, dtype=F16, parts=0):
            if parts:
                return [[room.take(size, dtype) for _ in range(parts)] for _ in range(n)]
            return [room.take(size, dtype) for _ in range(n)]

        x1_in = ring(2, H, F32)
        x1_part = ring(2, H, parts=2)
        x1b = ring(4, H, F32)
        bd1_f = room.take(GB * HID, F32)
        bd1 = ring(2, GB * HID, parts=2)
        bd2_f = room.take(GB * S, F32)
        bd2 = ring(2, GB * S, parts=2)
        hid_f = ring(2, H, F32)
        hid = [ring(2, H, parts=2) for _ in range(2)]
        c1_f = room.take(KH * P, F32)
        c1 = ring(2, KH * P, parts=2)
        lg = room.take(8, F32)
        mx8 = room.take(8, F32)
        ix8 = room.take(8, U32)
        gap = room.take(8, F32)
        th = room.take(8, F32)
        ixf = room.take(8, F32)
        pp = room.take(8, F32)
        e1x = [room.take(8, F32) for _ in range(3)]
        hw = room.take(P, F32)
        hwt = [room.take(P, F16) for _ in range(2)]
        x2_f = ring(2, H, F32)
        x2_part = ring(2, H, parts=2)
        x2b = ring(2, H, F32)
        c2 = ring(2, KH * P, parts=2)
        x3_f = ring(2, H, F32)
        room.at = c_start
        x3_in = ring(4, H, F32)
        x3b = ring(4, H, F32)
        w3_now = ring(2, KH * H, parts=2)
        row_now = [room.take(8, I32) for _ in range(4)]
        row_put = [room.take(8, I32) for _ in range(2)]
        x3t = ring(2, KH * P, parts=2)
        c3t = ring(2, KH * P, parts=2)
        sc8 = room.take(8, F32)
        mc8 = room.take(8, F32)
        ic8 = room.take(8, U32)
        icf = room.take(8, F32)
        negm = room.take(8, F32)
        ex = room.take(8, F32)
        esum = room.take(8, F32)
        rec = room.take(8, F32)
        wn = room.take(8, F32)
        keep = room.take(R3, F32)
        hl = room.take(P, F32)
        hlt = [room.take(P, F16) for _ in range(2)]
        fin = ring(2, H, F32)
        w3 = [w[:, 0:NLW].rearrange("p (a x) -> p a x", a=AD3) for w in w0]

        def late_weight(parts, table, name, k):
            at = sum(n for _, n in table[:[m for m, _ in table].index(name)])
            size = dict(table)[name]
            return [w[:, at:at + size].rearrange("p (k c) -> p k c", k=k) for w in parts]

        w_base1 = late_weight(wb_part, LATE_B, "base1", KH)
        w_ar1 = late_weight(wb_part, LATE_B, "ar1", KH)
        w_b1 = late_weight(wb_part, LATE_B, "b1", 1)
        w_mix1 = late_weight(wb_part, LATE_B, "mix1", 1)
        w_2 = [w.rearrange("p (k c) -> p k c", k=KH) for w in w2_part]
        w_base3 = late_weight(wc_part, LATE_C, "base3", KH)
        w_ag3 = late_weight(wc_part, LATE_C, "ag3", KH)
        w_b3 = late_weight(wc_part, LATE_C, "b3", 1)

        index_in = sem("index_in")
        const_in = sem("const_in")
        bias_in = sem("bias_in")
        index_ready = sem("index_ready")
        prep_loaded = [sem(f"prep_loaded{n}") for n in range(RING)]
        prep_hi = sem("prep_hi")
        prep_lo = sem("prep_lo")
        x_loaded = sem("x_loaded")
        pool_turns = sem("pool_turns")
        dve_turns = sem("dve_turns")
        x_hi = sem("x_hi")
        x_split = sem("x_split")
        index_copied = sem("index_copied")
        la_loaded = sem("la_loaded")
        lb_loaded = sem("lb_loaded")
        lora_hi = sem("lora_hi")
        lora_split = sem("lora_split")
        gate_ready = sem("gate_ready")
        up_ready = sem("up_ready")
        silu_done = sem("silu_done")
        prod_done = sem("prod_done")
        act_hi = sem("act_hi")
        act_split = sem("act_split")
        t_ready = sem("t_ready")
        t_step = sem("t_step")
        t_split = sem("t_split")
        down_ready = sem("down_ready")
        c0_hi = sem("c0_hi")
        c0_split = sem("c0_split")
        c0_stored = sem("c0_stored")
        dq_loaded = sem("dq_loaded")
        dq_bits = sem("dq_bits")
        dq_step = sem("dq_step")
        dq_split = sem("dq_split")
        wq_stored = sem("wq_stored")
        wq_loaded = [sem(f"wq_loaded{n}") for n in range(NF + 1)]
        ct_loaded = [sem(f"ct_loaded{n}") for n in range(2)]
        xn_loaded = [sem(f"xn_loaded{n}") for n in range(2)]
        gate2_ready = sem("gate2_ready")
        up2_ready = sem("up2_ready")
        silu2_done = sem("silu2_done")
        prod2_done = sem("prod2_done")
        act2_hi = sem("act2_hi")
        act2_split = sem("act2_split")
        down2_ready = sem("down2_ready")
        out16_done = sem("out16_done")
        x1_done = sem("x1_done")
        x1_stored = [sem(f"x1_stored{n}") for n in range(2)]

        table_step = sem("table_step")
        table_mm = sem("table_mm")
        late_loaded = sem("late_loaded")
        late_free = sem("late_free")
        late_hi = sem("late_hi")
        late_split = sem("late_split")
        late_stored = sem("late_stored")
        deq2_loaded = sem("deq2_loaded")
        deq2_step = sem("deq2_step")
        deq2_done = sem("deq2_done")
        mix_loaded = sem("mix_loaded")
        mix_ready = sem("mix_ready")
        wb_loaded = sem("wb_loaded")
        wc_loaded = sem("wc_loaded")
        w3_loaded = sem("w3_loaded")
        x1b_done = sem("x1b_done")
        bd1_step = sem("bd1_step")
        bd2_step = sem("bd2_step")
        x1_hi = sem("x1_hi")
        x1_split = sem("x1_split")
        bd1_ready = sem("bd1_ready")
        bd2_ready = sem("bd2_ready")
        hid_ready = sem("hid_ready")
        gelu_done = sem("gelu_done")
        hid_hi = sem("hid_hi")
        hid_split = sem("hid_split")
        mixed_ready = sem("mixed_ready")
        c1_step = sem("c1_step")
        c1_split = sem("c1_split")
        router_ready = sem("router_ready")
        r_step = sem("r_step")
        gap_ready = sem("gap_ready")
        tanh_done = sem("tanh_done")
        hw_done = sem("hw_done")
        hwt_ready = sem("hwt_ready")
        hwt_hi = sem("hwt_hi")
        hwt_split = sem("hwt_split")
        x2_ready = sem("x2_ready")
        x2_done = sem("x2_done")
        x2_hi = sem("x2_hi")
        x2_split = sem("x2_split")
        x2b_done = sem("x2b_done")
        c2_ready = sem("c2_ready")
        c2_hi = sem("c2_hi")
        c2_split = sem("c2_split")
        y3_ready = sem("y3_ready")
        x3_done = sem("x3_done")
        row_copied = sem("row_copied")
        row_put_copied = sem("row_put_copied")
        x3b_done = sem("x3b_done")
        xt3_ready = sem("xt3_ready")
        xt3_hi = sem("xt3_hi")
        xt3_split = sem("xt3_split")
        cond3_ready = sem("cond3_ready")
        w3_copied = sem("w3_copied")
        ct3_hi = sem("ct3_hi")
        ct3_split = sem("ct3_split")
        ag3_ready = sem("ag3_ready")
        g_step = sem("g_step")
        negm_ready = sem("negm_ready")
        exp_done = sem("exp_done")
        hl_done = sem("hl_done")
        hlt_ready = sem("hlt_ready")
        hlt_hi = sem("hlt_hi")
        hlt_split = sem("hlt_split")
        fin_ready = sem("fin_ready")
        fin_done = sem("fin_done")
        x1_loaded = [sem(f"x1_loaded{n}") for n in range(2)]
        x3_stored = [sem(f"x3_stored{n}") for n in range(2)]
        x3_loaded = [sem(f"x3_loaded{n}") for n in range(4)]
        fin_stored = [sem(f"fin_stored{n}") for n in range(2)]

        jobs = []
        for at in range(0, WFLAT, PREP):
            w = min(PREP, WFLAT - at)
            jobs.append((d["w_cond"][:, at:at + w], w, w0[0][:, at:at + w], w0[1][:, at:at + w]))
        AHEAD = 2
        job_after = {n: max((n - AHEAD) // 2, n - AHEAD - 6) for n in range(AHEAD, len(jobs))}
        assert max(job_after.values()) == 8 and LB // 2 >= FP + 2 * P

        def jobs_behind(f):
            return [n for n in range(AHEAD, len(jobs)) if job_after[n] == f]

        PIECES = 4

        def lora_piece(p, n):
            if n < 2:
                b = slice(n * BA // 2, (n + 1) * BA // 2)
                v = la[p].rearrange("p (h c b r) -> p h c b r", h=2, b=BA, r=RANK)
                return (la_raw.rearrange("p (b c r) -> p c b r", b=BA, r=RANK)[:, :, b],
                        v[:, 0, :, b], v[:, 1, :, b])
            at = (n - 2) * (LB // 2)
            return (lb_raw[:, at:at + LB // 2], lb[p][:, at:at + LB // 2], lb[p][:, LB + at:LB + at + LB // 2])

        CR_PROD = 2
        CR_DOWN = 8
        CR_C0 = 2
        CR_X = 1

        block = ctx.enter_context(nc.Block())

        def valid(i, first, end):
            return not isinstance(i, int) or first <= i < end

        def run_b(eng, step, between=None, beside=None):
            turns = (NG - 5 - 3) // 4
            for i in range(-4, 4):
                step(i, i % 4)
            if between:
                between()
            if beside:
                with eng.Fori(0, AD3 // 4) as it:
                    for u in range(4, 8):
                        step(it * 4 + u, u % 4)
                        beside(it * 4 + (u - 4))
            with eng.Fori(AD3 // 4 if beside else 0, turns) as it:
                for u in range(4, 8):
                    step(it * 4 + u, u % 4)
            for i in range(4 * turns + 4, NG + 2):
                step(i, i % 4)

        def run_c(eng, step):
            turns = (NCH - 5 - 2) // 4
            for i in range(-5, 2):
                step(i, i % 4)
            with eng.Fori(0, turns) as it:
                for u in range(2, 6):
                    step(it * 4 + u, u % 4)
            for i in range(4 * turns + 2, NCH):
                step(i, i % 4)

        def run_a(eng, tile):
            for i in range(2):
                tile(i, i)
            with eng.Fori(1, NA // 2 - 1) as it:
                for p in range(2):
                    tile(it * 2 + p, p)
            for i in range(NA - 2, NA):
                tile(i, i % 2)

        def pieces_behind(first):
            return {9: [0, 1], 10: [2, 3]} if first else {6: [0], 7: [1], 8: [2], 9: [3]}

        def slot_count(g, v, ring_size):
            return (g - v % ring_size) * (16 // ring_size) + 16

        def load_count(g, v):
            return slot_count(g, v, 2)

        def load_beside(sp, i):
            sp.wait_ge(late_split, i + 1)
            sp.dma_start(late_in, d["late"][:, bass.ds(i * LQ, LQ)]).then_inc(late_loaded, 16)
            sp.wait_ge(deq2_done, i + 1)
            for dst, name in ((p2_in, "p2"), (s2_in, "s2"), (m2_in, "m2")):
                sp.dma_start(dst, d[name][:, bass.ds(i * DQ2, DQ2)]).then_inc(deq2_loaded, 16)

        def load_ct(sp, i, p):
            for h in range(2):
                sp.dma_start(ct[p][h], c0[h][:, :, bass.ds(i * TB, TB)]).then_inc(ct_loaded[p], 16)

        def load_xn(sp, i, p):
            xn_in = d["x"].rearrange("(g p) h -> p g h", p=P)
            sp.dma_start(xn[p], xn_in[:, bass.ds(i * 4, 4), :]).then_inc(xn_loaded[p], 16)

        @block.sync
        def _(sp):
            sp.dma_start(ids[:, 0:NFIRST], d["ids"][:, 0:NFIRST]).then_inc(index_in, 16)
            sp.dma_start(consts[:, 0:2], d["consts"][:, 0:2]).then_inc(index_in, 16)
            sp.dma_start(consts[:, 2:NCONST], d["consts"][:, 2:NCONST]).then_inc(const_in, 16)
            sp.dma_start(shift, d["shift"]).then_inc(const_in, 16)
            sp.dma_start(ids[:, NFIRST:NIDS], d["ids"][:, NFIRST:NIDS]).then_inc(const_in, 16)
            sp.dma_start(b_sess, d["b_sess"]).then_inc(const_in, 16)

            def load_x(i):
                sp.dma_start(xs.rearrange("p (k t) -> p k t", k=KH),
                             d["xt"].rearrange("(k p) t -> p k t", p=P)[:, :, bass.ds(i * TA, TA)]
                             ).then_inc(x_loaded, 16)

            def load_dq(i):
                sp.dma_start(dq_q, d["q"][:, bass.ds(i * DQ, DQ)]).then_inc(dq_loaded, 16)
                sp.dma_start(dq_zp, d["z"][0:1, bass.ds(i * (DQ // 8), DQ // 8)].partition_broadcast(P)
                             ).then_inc(dq_loaded, 16)
                sp.dma_start(dq_s, d["s"][0:1, bass.ds(i * DQ, DQ)].partition_broadcast(P)).then_inc(dq_loaded, 16)

            load_x(0)
            for n, (src, w, _, _) in enumerate(jobs):
                if n == RING:
                    load_dq(0)
                    sp.dma_start(biases, d["biases"]).then_inc(bias_in, 16)
                if n == 1:
                    sp.wait_ge(la_loaded, 16 * BA)
                if n >= RING:
                    sp.wait_ge(prep_lo, n - RING + 1)
                sp.dma_start(prep_in[n % RING][:, 0:w], src).then_inc(prep_loaded[n % RING], 16)
            with sp.Fori(1, NA) as i:
                sp.wait_ge(x_split, i + 1)
                load_x(i)
                sp.wait_ge(dq_split, i + 1)
                load_dq(i)
            sp.wait_ge(up_ready, NF * NA)
            sp.wait_ge(wq_stored, 32 * -(-GU // DQ))
            sp.wait_ge(lora_split, PIECES * NA)
            sp.wait_ge(c0_stored, 32 * (TB // TA) + 32)
            for f in range(NF):
                for h in range(2):
                    sp.dma_start(w0[h][:, f * PREP:(f + 1) * PREP],
                                 wq[h, :, f * PREP:(f + 1) * PREP]).then_inc(wq_loaded[f], 16)
                if f == 0:
                    load_ct(sp, 0, 0)
            sp.wait_ge(down_ready, 4 * NA + CR_DOWN)
            sp.wait_ge(wq_stored, 32 * NA)
            for h in range(2):
                sp.dma_start(w0[h][:, GU:WFLAT], wq[h, :, GU:WFLAT]).then_inc(wq_loaded[NF], 16)
            sp.wait_ge(c0_stored, 32 * NA + 32)
            load_beside(sp, 0)
            load_xn(sp, 0, 0)
            load_ct(sp, 1, 1)
            load_xn(sp, 1, 1)
            load_beside(sp, 1)
            sp.wait_ge(late_stored, 32 * -(-NLB // LQ))
            for h in range(2):
                sp.dma_start(wb_part[h], late[h, :, 0:NLB]).then_inc(wb_loaded, 16)
            with sp.Fori(1, NB // 2) as it:
                for p in range(2):
                    sp.wait_ge(down2_ready, (it * 2 + p - 1) * 4)
                    load_ct(sp, it * 2 + p, p)
                    load_beside(sp, it * 2 + p)
                    sp.wait_ge(x1_stored[p], it * 64)
                    load_xn(sp, it * 2 + p, p)
            sp.wait_ge(late_stored, 32 * NB)
            for s in x1_stored:
                sp.wait_ge(s, 64)

            def step_b(i, u):
                g, v = i + 4, (u + 4) % 4
                if valid(g, 0, NG):
                    if valid(g - 2, 0, NG):
                        sp.wait_ge(x1b_done, g - 1)
                        sp.wait_ge(x1_split, g - 1)
                    sp.dma_start(x1_in[v % 2], x1[bass.ds(g * P, P), :]).then_inc(x1_loaded[v % 2], 16)
                g, v = i - 2, (u - 2) % 4
                if valid(g, 0, NG):
                    sp.wait_ge(x3_done, g + 1)
                    sp.dma_start(x3[bass.ds(g * P, P), :], x3_f[v % 2]).then_inc(x3_stored[v % 2], 16)

            def load_late():
                for s in x1_stored:
                    sp.wait_ge(s, 64 * NB // 2)
                sp.wait_ge(down2_ready, 4 * NB)
                for h in range(2):
                    sp.dma_start(wc_part[h], late[h, :, NLB:NLB + NLC]).then_inc(wc_loaded, 16)

            def load_w3(a):
                for h in range(2):
                    sp.dma_start(w3[h][:, bass.ds(a, 1), :].rearrange("p o x -> p (o x)"),
                                 late[h, :, bass.ds(NLB + NLC + a * (KH * H), KH * H)]).then_inc(w3_loaded, 16)

            run_b(sp, step_b, load_late, load_w3)

        @block.gpsimd
        def _(pool):
            pool.sem_inc(x_split, 1)
            pool.sem_inc(dq_split, 1)
            pool.sem_inc(x1_done, 4)
            pool.sem_inc(late_free, 1)
            pool.wait_ge(index_ready, 1)

            def pool_wait(on, value):
                pool.wait_ge(on, value)
                pool.sem_inc(pool_turns, 1)

            def prepare(i, p):
                pool.tensor_copy(index_now[p], index[:, bass.ds(i * NIX, NIX)]).then_inc(index_copied, 1)
                pool_wait(index_copied, i + 1)
                if valid(i, 1, NA):
                    pool_wait(lora_split, i * PIECES)
                for b in range(BA):
                    pool.indirect_dma_start(
                        la_raw[:, b * LA:(b + 1) * LA], None, d["lora_a"],
                        bass.IndirectOffsetOnAxis(ap=index_now[p][:, b:b + 1], axis=0)
                    ).then_inc(la_loaded, 16)
                pool.indirect_dma_start(
                    lb_raw, None, d["lora_b"],
                    bass.IndirectOffsetOnAxis(ap=index_now[p][:, BA:BA + 1], axis=0)
                ).then_inc(lb_loaded, 16)
                pool_wait(down_ready, i * 4 + 4)
                pool_wait(x_loaded, (i + 1) * 16)
                pool.tensor_copy(xt[p][0], xs).then_inc(x_hi, 1)
                pool_wait(x_hi, i + 1)
                pool.tensor_tensor(xt[p][1], xs, xt[p][0], ALU.subtract).then_inc(x_split, 1)

            def dequantise(i):
                pool_wait(dq_bits, (i + 1) * 2)
                pool.tensor_scalar(dq_n, dq_n, -1.0, WS, ALU.add, ALU.mult).then_inc(dq_step, 1)
                pool_wait(dq_step, i * 3 + 1)
                pool.tensor_tensor(dq_n, dq_n, dq_s, ALU.mult).then_inc(dq_step, 1)
                pool_wait(dq_step, i * 3 + 2)
                pool.tensor_copy(dq_part[0], dq_n).then_inc(dq_step, 1)
                pool_wait(dq_step, i * 3 + 3)
                pool.tensor_tensor(dq_part[1], dq_n, dq_part[0], ALU.subtract).then_inc(dq_split, 1)
                pool_wait(dq_split, i + 2)
                for h in range(2):
                    pool.dma_start(wq[h, :, bass.ds(i * DQ, DQ)], dq_part[h]).then_inc(wq_stored, 16)
                pool_wait(wq_stored, i * 32 + 32)

            prepare(0, 0)
            with pool.Fori(0, NA // 2 - 1) as it:
                for p in range(2):
                    prepare(it * 2 + p + 1, 1 - p)
                    dequantise(it * 2 + p)
            prepare(NA - 1, 1)
            dequantise(NA - 2)
            dequantise(NA - 1)
            pool.wait_ge(down_ready, 4 * NA + CR_DOWN)
            for g in range(NG):
                for n, (dst, width, table) in enumerate(((mix1, HID, d["w_sess"]), (mix2, S, d["w_mix2"]))):
                    pool.indirect_dma_start(
                        dst[:, g * width:(g + 1) * width], None, table,
                        bass.IndirectOffsetOnAxis(ap=index1[:, n * NG + g:n * NG + g + 1], axis=0)
                    ).then_inc(mix_loaded, 16)
            pool.wait_ge(mix_loaded, 32 * NG)
            for g in range(NG):
                v = mix1[:, g * HID:(g + 1) * HID]
                pool.tensor_scalar(v, v, clen[:, g:g + 1], None, ALU.mult)
            pool.tensor_scalar(mix2, mix2, WS, None, ALU.mult).then_inc(mix_ready, 1)
            x1_out = x1.rearrange("(g p) h -> p g h", p=P)
            with pool.Fori(0, NB // 2) as it:
                for p in range(2):
                    i = it * 2 + p
                    pool_wait(late_split, i + 2)
                    for h in range(2):
                        pool.dma_start(late[h, :, bass.ds(i * LQ, LQ)], late_part[h]).then_inc(late_stored, 16)
                    pool_wait(xn_loaded[p], (it + 1) * 16)
                    for g in range(4):
                        pool_wait(out16_done, i * 4 + g + 5)
                        pool.tensor_tensor(xn[p][:, g, :], xn[p][:, g, :], out16[g % 2], ALU.add).then_inc(x1_done, 1)
                        pool_wait(x1_done, i * 4 + g + 5)
                        pool.dma_start(x1_out[:, bass.ds(i * 4 + g, 1), :], xn[p][:, g:g + 1, :]).then_inc(x1_stored[p], 16)
                    pool_wait(late_stored, i * 32 + 32)
                    pool.sem_inc(late_free, 1)
            pool.wait_ge(mix_ready, 1)
            pool.wait_ge(bias_in, 16)
            blocks = const("blocks").rearrange("p (q o) -> p q o", o=1)

            def block_diagonal(rows, g, width, f, parts, ready, step):
                row = rows[:, bass.ds(g * width, width)].rearrange("p (o c) -> p o c", o=1)
                pool.tensor_tensor(f.rearrange("p (q c) -> p q c", q=GB), row.broadcast_to((P, GB, width)),
                                   blocks.broadcast_to((P, GB, width)), ALU.mult).then_inc(step, 1)
                pool_wait(step, 2 * g + 1)
                pool.tensor_copy(parts[0], f).then_inc(step, 1)
                pool_wait(step, 2 * g + 2)
                pool.tensor_tensor(parts[1], f, parts[0], ALU.subtract).then_inc(ready, 1)

            def step_b(i, u):
                g, v = i + 3, (u + 3) % 4
                if valid(g, 0, NG):
                    pool_wait(x1_hi, g + 1)
                    pool.tensor_tensor(x1_part[v % 2][1], x1_in[v % 2], x1_part[v % 2][0], ALU.subtract
                                       ).then_inc(x1_split, 1)
                    if valid(g - 1, 0, NG):
                        pool_wait(bd1_ready, g)
                    if valid(g - 2, 0, NG):
                        pool_wait(hid_ready, 2 * (g - 1))
                    block_diagonal(mix1, g, HID, bd1_f, bd1[v % 2], bd1_ready, bd1_step)
                    if valid(g - 4, 0, NG):
                        pool_wait(x2_done, g - 3)
                    pool.tensor_tensor(x1b[v], x1_in[v % 2], bias_of("base1"), ALU.add).then_inc(x1b_done, 1)
                g, v = i, u
                if valid(g, 0, NG):
                    if valid(g - 2, 0, NG):
                        pool_wait(c2_ready, g - 1)
                    if valid(g - 1, 0, NG):
                        pool_wait(bd2_ready, g)
                    block_diagonal(mix2, g, S, bd2_f, bd2[v % 2], bd2_ready, bd2_step)
                    pool_wait(x2_done, g + 1)
                    pool_wait(x2_hi, g + 1)
                    pool.tensor_tensor(x2_part[v % 2][1], x2_f[v % 2], x2_part[v % 2][0], ALU.subtract
                                       ).then_inc(x2_split, 1)
                    if valid(g - 2, 0, NG):
                        pool_wait(x3_done, g - 1)
                    pool.tensor_tensor(x2b[v % 2], x2_f[v % 2], bias_of("ffn2"), ALU.add).then_inc(x2b_done, 1)

            run_b(pool, step_b)
            for s in x3_stored:
                pool.wait_ge(s, 16 * NG // 2)

            def step_c(i, u):
                j, v = i + 5, (u + 5) % 4
                if valid(j, 0, NCH):
                    if valid(j - 4, 0, NCH):
                        pool_wait(xt3_ready, j - 3)
                        pool_wait(x3b_done, j - 3)
                    pool.tensor_copy(row_now[v][:, 0:1], rows_in[:, bass.ds(j, 1)]).then_inc(row_copied, 1)
                    pool_wait(row_copied, j + 1)
                    pool.indirect_dma_start(x3_in[v], None, x3,
                                            bass.IndirectOffsetOnAxis(ap=row_now[v][:, 0:1], axis=0)
                                            ).then_inc(x3_loaded[v], 16)
                j, v = i + 3, (u + 3) % 4
                if valid(j, 0, NCH):
                    pool_wait(x3_loaded[v], slot_count(j, v, 4))
                    if valid(j - 4, 0, NCH):
                        pool_wait(fin_done, j - 3)
                    pool.tensor_tensor(x3b[v], x3_in[v], bias_of("base3"), ALU.add).then_inc(x3b_done, 1)
                j, v = i, u
                if valid(j, 0, NCH):
                    if valid(j - 2, 0, NCH):
                        pool_wait(fin_stored[v % 2], slot_count(j - 2, v, 2))
                    pool.tensor_copy(row_put[v % 2][:, 0:1], rows_out[:, bass.ds(j, 1)]).then_inc(row_put_copied, 1)
                    pool_wait(row_put_copied, j + 1)
                    pool_wait(fin_done, j + 1)
                    pool.indirect_dma_start(out, bass.IndirectOffsetOnAxis(ap=row_put[v % 2][:, 0:1], axis=0),
                                            fin[v % 2], None, bounds_check=TOK - 1, oob_is_err=False
                                            ).then_inc(fin_stored[v % 2], 16)

            run_c(pool, step_c)
            for n in range(2):
                pool.wait_ge(fin_stored[n], 16 * ((NCH + 1 - n) // 2))

        @block.scalar
        def _(act_e):
            act_e.sem_inc(c0_stored, 32)
            act_e.sem_inc(out16_done, 4)

            def weights_hi(n):
                _, w, hi, _ = jobs[n]
                act_e.wait_ge(prep_loaded[n % RING], 16 * (n // RING + 1))
                act_e.activation(hi, prep_in[n % RING][:, 0:w], ACT.Copy, scale=WS).then_inc(prep_hi, 1)

            def lora_hi_of(i, p, n):
                act_e.wait_ge(*((la_loaded, (i + 1) * 16 * BA) if n < 2 else (lb_loaded, (i + 1) * 16)))
                raw, hi, _ = lora_piece(p, n)
                act_e.activation(hi, raw, ACT.Copy, scale=WS).then_inc(lora_hi, 1)

            def tile(i, p):
                for f in range(NF):
                    q = (p + f) % 2
                    act_e.wait_ge(gate_ready, i * NF + f + 1)
                    act_e.wait_ge(prod_done, i * NF + f + 1)
                    act_e.activation(sil[q], bank[q][:, 0:TA], ACT.Silu, scale=IWS).then_inc(silu_done, 1)
                    first = isinstance(i, int) and i == 0
                    for n in jobs_behind(f) if first else []:
                        weights_hi(n)
                    if first and f == 9:
                        act_e.wait_ge(prep_lo, len(jobs))
                    if valid(i, 0, NA - 1) and f in pieces_behind(first):
                        for n in pieces_behind(first)[f]:
                            lora_hi_of(i + 1, 1 - p, n)
                act_e.wait_ge(c0_split, (i + 1) * 4 + CR_C0)
                for h in range(2):
                    act_e.dma_start(c0[h][:, :, bass.ds(i * TA, TA)], c0_part[h]).then_inc(c0_stored, 16)

            for n in range(PIECES):
                if n == 2:
                    weights_hi(0)
                lora_hi_of(0, 0, n)
            weights_hi(1)
            run_a(act_e, tile)
            act_e.wait_ge(c0_stored, 32 * NA + 32)
            act_e.wait_ge(dq_split, NA + 1)
            with act_e.Fori(0, NB // 2) as it:
                for p in range(2):
                    i = it * 2 + p
                    for f in range(NF):
                        q = (p + f) % 2
                        act_e.wait_ge(gate2_ready, i * NF + f + 1)
                        act_e.wait_ge(prod2_done, i * NF + f + 1)
                        act_e.activation(sil2[q], bank[q][:, :], ACT.Silu, scale=IWS).then_inc(silu2_done, 1)
                        if f == 3:
                            act_e.wait_ge(late_loaded, i * 16 + 16)
                            act_e.wait_ge(late_free, i + 1)
                            act_e.activation(late_part[0], late_in, ACT.Copy, scale=WS).then_inc(late_hi, 1)
                    for g in range(4):
                        act_e.wait_ge(down2_ready, i * 4 + g + 1)
                        act_e.wait_ge(x1_done, i * 4 + g + 3)
                        act_e.activation(out16[g % 2], bank[4 + g][:, :], ACT.Copy, scale=IWS).then_inc(out16_done, 1)

            def step_b(i, u):
                g, v = i + 3, (u + 3) % 4
                if valid(g, 0, NG):
                    act_e.wait_ge(x1_loaded[v % 2], load_count(g, v))
                    if valid(g - 2, 0, NG):
                        act_e.wait_ge(hid_ready, 2 * (g - 1))
                    act_e.activation(x1_part[v % 2][0], x1_in[v % 2], ACT.Copy).then_inc(x1_hi, 1)
                g, v = i - 1, (u - 1) % 4
                if valid(g, 0, NG):
                    act_e.wait_ge(c2_ready, g + 1)
                    act_e.activation(c2[v % 2][0], bank[6][:, :], ACT.Copy, scale=IWS).then_inc(c2_hi, 1)
                g, v = i, u
                if valid(g, 0, NG):
                    act_e.wait_ge(gap_ready, g + 1)
                    act_e.activation(th[:, 0:1], gap[:, 0:1], ACT.Tanh, scale=0.5).then_inc(tanh_done, 1)
                g, v = i + 2, (u + 2) % 4
                if valid(g, 0, NG):
                    for pair in range(2):
                        act_e.wait_ge(hid_ready, 2 * g + pair + 1)
                        if valid(g - 1, 0, NG):
                            act_e.wait_ge(hid_split, 2 * g + pair - 1)
                        act_e.activation(hid_f[pair], bank[pair][:, :], ACT.Gelu,
                                         bias=bias_hid[:, bass.ds(g * 2 + pair, 1)], scale=IWS).then_inc(gelu_done, 1)
                    for pair in range(2):
                        act_e.wait_ge(gelu_done, 2 * g + pair + 1)
                        if valid(g - 2, 0, NG):
                            act_e.wait_ge(mixed_ready, g - 1)
                        act_e.activation(hid[v % 2][pair][0], hid_f[pair], ACT.Copy).then_inc(hid_hi, 1)
                g, v = i, u
                if valid(g, 0, NG):
                    act_e.wait_ge(x2_done, g + 1)
                    if valid(g - 2, 0, NG):
                        act_e.wait_ge(c2_ready, g - 1)
                    act_e.activation(x2_part[v % 2][0], x2_f[v % 2], ACT.Copy).then_inc(x2_hi, 1)

            run_b(act_e, step_b)

            def step_c(i, u):
                j, v = i, u
                if valid(j, 0, NCH):
                    act_e.wait_ge(negm_ready, j + 1)
                    act_e.activation(ex[:, 0:NR3], sc8[:, 0:NR3], ACT.Exp, bias=negm[:, 0:1],
                                     accum_out=esum[:, 0:1]).then_inc(exp_done, 1)
                j, v = i + 1, (u + 1) % 4
                if valid(j, 0, NCH):
                    act_e.wait_ge(cond3_ready, j + 1)
                    if valid(j - 2, 0, NCH):
                        act_e.wait_ge(ag3_ready, 2 * (j - 1))
                    act_e.activation(c3t[v % 2][0], bank[1][:, :], ACT.Copy, scale=IWS).then_inc(ct3_hi, 1)
                j, v = i + 2, (u + 2) % 4
                if valid(j, 0, NCH):
                    act_e.wait_ge(xt3_ready, j + 1)
                    if valid(j - 2, 0, NCH):
                        act_e.wait_ge(cond3_ready, j - 1)
                    act_e.activation(x3t[v % 2][0], bank[0][:, :], ACT.Copy).then_inc(xt3_hi, 1)

            run_c(act_e, step_c)

        @block.vector
        def _(dve):
            dve.sem_inc(prod_done, CR_PROD)
            dve.sem_inc(c0_split, CR_C0)
            dve.sem_inc(prod2_done, CR_PROD)
            dve.sem_inc(late_split, 1)
            dve.sem_inc(deq2_done, 1)
            dve.wait_ge(index_in, 32)
            ix = index_f.rearrange("p (t c) -> p t c", c=NIX)
            idv = ids_of("lora0").rearrange("p (t b) -> p t b", b=BA)
            dve.tensor_scalar(ix[:, :, 0:BA], idv, float(P), const("col"), ALU.mult, ALU.add).then_inc(t_step, 1)
            dve.tensor_scalar(ix[:, :, BA:NIX], ids_of("lora0_own").rearrange("p (t o) -> p t o", o=1),
                              float(RANK), const("mod16"), ALU.mult, ALU.add).then_inc(t_step, 1)
            dve.wait_ge(t_step, 2)
            dve.tensor_copy(index, index_f).then_inc(index_ready, 1)

            steps = [0]

            def table(ins):
                steps[0] += 1
                ins.then_inc(table_step, 1)
                dve.wait_ge(table_step, steps[0])

            def make_tables():
                dve.wait_ge(const_in, 64)
                col = const("col")
                table(dve.tensor_copy(ids_f, ids))

                def idf(name):
                    return ids_f[:, IDS[name][0]:IDS[name][0] + IDS[name][1]]

                for n, name in enumerate(("sess_own", "cond_own")):
                    table(dve.tensor_scalar(row1_f[:, n * NG:(n + 1) * NG], idf(name), float(S), const("mod32"),
                                            ALU.mult, ALU.add))
                table(dve.tensor_copy(index1, row1_f))
                table(dve.tensor_scalar(clen, idf("len_own"), const("mod32"), WS, ALU.is_gt, ALU.mult))
                for k in range(KH):
                    table(dve.tensor_scalar(tmask[:, k, :], idf("seq"), const("hcol")[:, k:k + 1], None, ALU.is_gt))
                table(dve.tensor_scalar(onehot, idf("sess"), col, None, ALU.is_equal))
                dve.wait_ge(table_mm, 1)
                for half in range(2):
                    at = slice(half * HID, (half + 1) * HID)
                    table(dve.tensor_copy(bias_hid[at, :], bank[7][at, 0:B].rearrange("p (n t) -> p n t", t=2)[:, :, half]))
                table(dve.tensor_scalar(onehot, idf("adapter"), col, None, ALU.is_equal))
                table(dve.tensor_reduce(count[:, 0:1], onehot, AX_X, ALU.add))
                table(dve.tensor_scalar(count_i[:, 0:1], count[:, 0:1], float(GB - 1), None, ALU.add))
                table(dve.tensor_scalar(count_i[:, 1:2], count_i[:, 0:1], 2, 2, ALU.logical_shift_right,
                                        ALU.logical_shift_left))
                table(dve.tensor_copy(count[:, 1:2], count_i[:, 1:2]))
                table(dve.tensor_scalar(spread, const("ones"), count[:, 1:2], None, ALU.mult))
                table(dve.tensor_scalar(later, idf("adapter"), col, None, ALU.is_gt))
                table(dve.scalar_tensor_tensor(same, idf("adapter"), idf("adapter_own"), const("before"),
                                               ALU.is_equal, ALU.mult))
                table(dve.tensor_scalar(own_adapter, const("ones")[:, 0:P], idf("adapter_own"), None, ALU.mult))
                dve.wait_ge(table_mm, 2)
                table(dve.tensor_tensor(at_batch, bank[6][:, 0:NCH * GB], const("places"), ALU.is_equal))
                dve.wait_ge(table_mm, 3)
                def by_place(v):
                    return v.rearrange("p (j q) -> p j q", q=GB)
                table(dve.tensor_tensor(by_place(chosen), by_place(bank[7][:, 0:NCH * GB]),
                                        const("blocks").rearrange("p (o q) -> p o q", o=1).broadcast_to((P, NCH, GB)),
                                        ALU.mult))
                table(dve.tensor_reduce(at_place, by_place(chosen), AX_X, ALU.add))
                table(dve.tensor_copy(adapter, by_place(bank[7][:, NCH * GB:2 * NCH * GB])[:, :, 0]))
                table(dve.tensor_scalar(row_f, at_place, -1.0, 0.0, ALU.add, ALU.max))
                table(dve.tensor_scalar(row_f, row_f, float(S), const("mod32"), ALU.mult, ALU.add))
                table(dve.tensor_copy(rows_in, row_f))
                table(dve.tensor_scalar(empty, at_place, 0.5, float(NO_ROW), ALU.is_lt, ALU.mult))
                table(dve.tensor_tensor(row_f, row_f, empty, ALU.add))
                table(dve.tensor_copy(rows_out, row_f))

            def weights_lo(n):
                _, w, hi, lo = jobs[n]
                dve.wait_ge(prep_hi, n + 1)
                dve.scalar_tensor_tensor(lo, prep_in[n % RING][:, 0:w], WS, hi, ALU.mult, ALU.subtract).then_inc(prep_lo, 1)

            def lora_lo_of(i, p, n):
                dve.wait_ge(lora_hi, i * PIECES + n + 1)
                raw, hi, lo = lora_piece(p, n)
                if n < 2:
                    for b in range(BA // 2):
                        ins = dve.scalar_tensor_tensor(lo[:, :, b], raw[:, :, b], WS, hi[:, :, b], ALU.mult, ALU.subtract)
                else:
                    ins = dve.scalar_tensor_tensor(lo, raw, WS, hi, ALU.mult, ALU.subtract)
                ins.then_inc(lora_split, 1)

            make_tables()
            for n in range(PIECES - 1):
                if n == 2:
                    weights_lo(0)
                lora_lo_of(0, 0, n)

            def t_parts(i, kind, src):
                dve.wait_ge(t_ready, i * 3 + kind + 1)
                dve.scalar_tensor_tensor(tf, src, 0.5 * IWS, own_batch, ALU.mult, ALU.mult).then_inc(t_step, 1)
                dve.wait_ge(t_step, i * 6 + 2 * kind + 1 + 2)
                dve.tensor_copy(t_part[kind][0], tf).then_inc(t_step, 1)
                dve.wait_ge(t_step, i * 6 + 2 * kind + 2 + 2)
                dve.tensor_tensor(t_part[kind][1], tf, t_part[kind][0], ALU.subtract).then_inc(t_split, 1)
                dve.wait_ge(t_split, i * 3 + kind + 1)

            def act_parts(i, f, p):
                q = (p + f) % 2
                dve.wait_ge(up_ready, i * NF + f + 1)
                dve.wait_ge(silu_done, i * NF + f + 1)
                dve.scalar_tensor_tensor(prod[q], bank[2 + q][:, 0:TA], IWS, sil[q], ALU.mult, ALU.mult).then_inc(prod_done, 1)
                dve.wait_ge(prod_done, i * NF + f + 1 + CR_PROD)
                dve.tensor_copy(act[0][:, f, :], prod[q]).then_inc(act_hi, 1)
                dve.wait_ge(act_hi, i * NF + f + 1)
                dve.tensor_tensor(act[1][:, f, :], prod[q], act[0][:, f, :], ALU.subtract).then_inc(act_split, 1)

            def tile(i, p):
                first = isinstance(i, int) and i == 0
                t_parts(i, 0, bank[4][:, 0:TA])
                t_parts(i, 1, bank[5][:, 0:TA])
                if first:
                    lora_lo_of(0, 0, PIECES - 1)
                    weights_lo(1)
                for f in range(NF):
                    act_parts(i, f, p)
                    for n in jobs_behind(f) if first else []:
                        weights_lo(n)
                    if f == 1:
                        dve.wait_ge(dq_loaded, (i + 1) * 48)
                        dve.tensor_scalar(dq_q, dq_q, shift[:, 0:1], 15, ALU.logical_shift_right,
                                          ALU.bitwise_and)
                    for j in range(2 * (f - 2), 2 * (f - 1)) if 2 <= f < 6 else []:
                        ins = dve.tensor_scalar(dq_z.rearrange("p (n j) -> p n j", j=8)[:, :, j], dq_zp,
                                                4 * j, 15, ALU.logical_shift_right, ALU.bitwise_and)
                        if j == 7:
                            ins.then_inc(dq_bits, 1)
                            dve.wait_ge(dq_bits, i * 2 + 1)
                            dve.tensor_tensor(dq_n, dq_q, dq_z, ALU.subtract).then_inc(dq_bits, 1)
                    if valid(i, 0, NA - 1) and f in pieces_behind(first):
                        for n in pieces_behind(first)[f]:
                            lora_lo_of(i + 1, 1 - p, n)
                t_parts(i, 2, bank[4][:, 0:TA])
                dve.wait_ge(c0_stored, i * 32 + 32)
                for hc in range(KH):
                    dve.wait_ge(down_ready, i * 4 + hc + 1 + CR_DOWN)
                    src = bank[6 + hc % 2][:, 0:TA]
                    dve.tensor_scalar(c0_part[0][:, hc, :], src, IWS, None, ALU.mult).then_inc(c0_hi, 1)
                    dve.wait_ge(c0_hi, i * 4 + hc + 1)
                    dve.scalar_tensor_tensor(c0_part[1][:, hc, :], src, IWS, c0_part[0][:, hc, :],
                                             ALU.mult, ALU.subtract).then_inc(c0_split, 1)

            run_a(dve, tile)
            dve.wait_ge(dq_split, NA + 1)

            def deq2(i):
                def step(ins, n):
                    ins.then_inc(deq2_step, 1)
                    dve.wait_ge(deq2_step, i * 6 + n)

                here = bass.ds(i * DQ2, DQ2)
                dve.wait_ge(deq2_loaded, i * 48 + 48)
                step(dve.tensor_scalar(p2_in, p2_in, shift[:, 1:2], 15, ALU.logical_shift_right, ALU.bitwise_and), 1)
                step(dve.tensor_scalar(n2, p2_in, -8.0, WS, ALU.add, ALU.mult), 2)
                step(dve.tensor_scalar(e2, m2_in, 0.5, 0.5, ALU.mult, ALU.add), 3)
                step(dve.tensor_tensor(e2, e2, s2_in, ALU.mult), 4)
                step(dve.tensor_tensor(n2, n2, e2, ALU.mult), 5)
                step(dve.tensor_copy(w2_part[0][:, here], n2), 6)
                dve.tensor_tensor(w2_part[1][:, here], n2, w2_part[0][:, here], ALU.subtract).then_inc(deq2_done, 1)
                dve.wait_ge(deq2_done, i + 2)

            with dve.Fori(0, NB // 2) as it:
                for p in range(2):
                    i = it * 2 + p
                    for f in range(NF):
                        q = (p + f) % 2
                        n = i * NF + f
                        dve.wait_ge(up2_ready, n + 1)
                        dve.wait_ge(silu2_done, n + 1)
                        dve.scalar_tensor_tensor(prod2[q], bank[2 + q][:, :], IWS, sil2[q], ALU.mult,
                                                 ALU.mult).then_inc(prod2_done, 1)
                        dve.wait_ge(prod2_done, n + 1 + CR_PROD)
                        dve.tensor_copy(act2[0][:, f, :], prod2[q]).then_inc(act2_hi, 1)
                        dve.wait_ge(act2_hi, n + 1)
                        dve.tensor_tensor(act2[1][:, f, :], prod2[q], act2[0][:, f, :], ALU.subtract
                                          ).then_inc(act2_split, 1)
                        if f == 4:
                            dve.wait_ge(late_hi, i + 1)
                            dve.scalar_tensor_tensor(late_part[1], late_in, WS, late_part[0], ALU.mult,
                                                     ALU.subtract).then_inc(late_split, 1)
                        if f == 6:
                            deq2(i)

            dve.wait_ge(bias_in, 16)
            def hid_lo(g, v, pair):
                if valid(g, 0, NG):
                    dve.wait_ge(hid_hi, 2 * g + pair + 1)
                    dve.tensor_tensor(hid[v % 2][pair][1], hid_f[pair], hid[v % 2][pair][0], ALU.subtract
                                      ).then_inc(hid_split, 1)

            def step_b(i, u):
                g = i
                if valid(g, 0, NG):
                    dve.wait_ge(router_ready, g + 1)
                    dve.tensor_scalar(lg, bank[4][:, EXP * R1:WAR], IWS, None, ALU.mult).then_inc(r_step, 1)
                hid_lo(i + 1, (u + 1) % 4, 0)
                if valid(g, 0, NG):
                    dve.wait_ge(r_step, g * 8 + 1)
                    dve.sem_inc(dve_turns, 1)
                    dve.max(mx8, lg).then_inc(r_step, 1)
                hid_lo(i + 1, (u + 1) % 4, 1)
                if valid(g, 0, NG):
                    dve.wait_ge(r_step, g * 8 + 2)
                    dve.sem_inc(dve_turns, 1)
                    dve.max_index(ix8, mx8, lg).then_inc(r_step, 1)
                    dve.tensor_tensor(gap[:, 0:1], mx8[:, 0:1], mx8[:, 1:2], ALU.subtract).then_inc(gap_ready, 1)
                    dve.wait_ge(r_step, g * 8 + 3)
                    dve.tensor_copy(ixf[:, 0:2], ix8[:, 0:2]).then_inc(r_step, 1)
                    dve.wait_ge(r_step, g * 8 + 4)
                    dve.wait_ge(tanh_done, g + 1)
                    dve.scalar_tensor_tensor(pp[:, 0:2], const("sign"), th[:, 0:1], const("one"), ALU.mult,
                                             ALU.add).then_inc(r_step, 1)
                    dve.wait_ge(r_step, g * 8 + 5)
                    for n in range(2):
                        dve.tensor_scalar(e1x[n], const("iota8"), ixf[:, n:n + 1], pp[:, n:n + 1], ALU.is_equal,
                                          ALU.mult).then_inc(r_step, 1)
                    dve.wait_ge(r_step, g * 8 + 7)
                    dve.tensor_tensor(e1x[2], e1x[0], e1x[1], ALU.add).then_inc(r_step, 1)
                    dve.wait_ge(r_step, g * 8 + 8)
                    if valid(g - 1, 0, NG):
                        dve.wait_ge(hwt_ready, g)
                    dve.scalar_tensor_tensor(
                        hw.rearrange("p (e r) -> p e r", e=EXP), bank[4][:, 0:EXP * R1].rearrange("p (e r) -> p e r", e=EXP),
                        IWS, e1x[2].rearrange("p (e o) -> p e o", o=1).broadcast_to((P, EXP, R1)), ALU.mult, ALU.mult
                    ).then_inc(hw_done, 1)
                g, v = i - 1, (u - 1) % 4
                if valid(g, 0, NG):
                    dve.wait_ge(c2_hi, g + 1)
                    dve.scalar_tensor_tensor(c2[v % 2][1], bank[6][:, :], IWS, c2[v % 2][0], ALU.mult, ALU.subtract
                                             ).then_inc(c2_split, 1)
                if valid(i, 0, NG):
                    dve.wait_ge(hwt_ready, i + 1)
                    dve.tensor_copy(hwt[0], bank[5][:, 0:P]).then_inc(hwt_hi, 1)
                g, v = i - 2, (u - 2) % 4
                if valid(g, 0, NG):
                    dve.wait_ge(y3_ready, g + 1)
                    dve.wait_ge(x2b_done, g + 1)
                    if valid(g - 2, 0, NG):
                        dve.wait_ge(x3_stored[v % 2], slot_count(g - 2, v, 2))
                    dve.scalar_tensor_tensor(x3_f[v % 2], bank[7][:, :], IWS, x2b[v % 2], ALU.mult, ALU.add
                                             ).then_inc(x3_done, 1)
                if valid(i, 0, NG):
                    dve.wait_ge(hwt_hi, i + 1)
                    dve.tensor_tensor(hwt[1], bank[5][:, 0:P], hwt[0], ALU.subtract).then_inc(hwt_split, 1)
                g, v = i + 1, (u + 1) % 4
                if valid(g, 0, NG):
                    dve.wait_ge(mixed_ready, g + 1)
                    c1v = c1_f.rearrange("p (n s) -> p n s", s=S)
                    dve.scalar_tensor_tensor(
                        c1v, bank[2][:, :].rearrange("p (n s) -> p n s", s=S), IWS,
                        bias_of("mix1").rearrange("p (o s) -> p o s", o=1).broadcast_to((P, KH * GB, S)),
                        ALU.mult, ALU.add).then_inc(c1_step, 1)
                    dve.wait_ge(c1_step, g * 3 + 1)
                    c1m = c1_f.rearrange("p (k b s) -> p k b s", k=KH, b=GB)
                    dve.tensor_tensor(c1m, c1m, tmask[:, :, bass.ds(g * GB, GB)].rearrange(
                        "p k (b o) -> p k b o", o=1).broadcast_to((P, KH, GB, S)), ALU.mult).then_inc(c1_step, 1)
                g, v = i, u
                if valid(g, 0, NG):
                    dve.wait_ge(x2_ready, g + 1)
                    dve.wait_ge(x1b_done, g + 1)
                    if valid(g - 2, 0, NG):
                        dve.wait_ge(x2b_done, g - 1)
                    dve.scalar_tensor_tensor(x2_f[v % 2], bank[3][:, :], IWS, x1b[v], ALU.mult, ALU.add
                                             ).then_inc(x2_done, 1)
                g, v = i + 1, (u + 1) % 4
                if valid(g, 0, NG):
                    dve.wait_ge(c1_step, g * 3 + 2)
                    dve.tensor_copy(c1[v % 2][0], c1_f).then_inc(c1_step, 1)
                    dve.wait_ge(c1_step, g * 3 + 3)
                    dve.tensor_tensor(c1[v % 2][1], c1_f, c1[v % 2][0], ALU.subtract).then_inc(c1_split, 1)

            run_b(dve, step_b)
            dve.wait_ge(x2b_done, NG)
            for s in x3_stored:
                dve.wait_ge(s, 16 * NG // 2)
            dve.wait_ge(w3_loaded, 32 * AD3)
            dve.memset(sc8, -3.0e38)
            dve.memset(hl, 0.0).then_inc(g_step, 1)
            dve.wait_ge(g_step, 1)

            def copy_w3(j, v):
                if valid(j - 2, 0, NCH):
                    dve.wait_ge(cond3_ready, j - 1)
                which = dve.value_load(adapter[0:1, bass.ds(j, 1)], min_val=0, max_val=AD3 - 1)
                for h in range(2):
                    dve.tensor_copy(w3_now[v][h].rearrange("p (o x) -> p o x", o=1),
                                    w3[h][:, bass.ds(which, 1), :]).then_inc(w3_copied, 1)

            for j in range(2):
                copy_w3(j, j)

            def step_c(i, u):
                j = i
                if valid(j, 0, NCH):
                    dve.wait_ge(ag3_ready, 2 * j + 1)
                    dve.scalar_tensor_tensor(sc8[:, 0:NR3], bank[4][:, R3:WAG], IWS, bias_of("gate3"), ALU.mult,
                                             ALU.add).then_inc(g_step, 1)
                    dve.wait_ge(g_step, j * 8 + 2)
                    dve.sem_inc(dve_turns, 1)
                    dve.max(mc8, sc8).then_inc(g_step, 1)
                    dve.wait_ge(g_step, j * 8 + 3)
                    dve.tensor_scalar(negm[:, 0:1], mc8[:, 0:1], -1.0, None, ALU.mult).then_inc(negm_ready, 1)
                    dve.max_index(ic8, mc8, sc8).then_inc(g_step, 1)
                    dve.wait_ge(g_step, j * 8 + 4)
                    dve.tensor_copy(icf[:, 0:1], ic8[:, 0:1]).then_inc(g_step, 1)
                    dve.wait_ge(exp_done, j + 1)
                    dve.reciprocal(rec[:, 0:1], esum[:, 0:1]).then_inc(g_step, 1)
                    dve.wait_ge(g_step, j * 8 + 6)
                    dve.reciprocal(wn[:, 1:2], rec[:, 0:1]).then_inc(g_step, 1)
                    dve.wait_ge(g_step, j * 8 + 7)
                    dve.tensor_tensor(wn[:, 0:1], rec[:, 0:1], wn[:, 1:2], ALU.mult).then_inc(g_step, 1)
                    dve.wait_ge(g_step, j * 8 + 8)
                    dve.tensor_scalar(keep, const("level"), icf[:, 0:1], wn[:, 0:1], ALU.is_le, ALU.mult
                                      ).then_inc(g_step, 1)
                    dve.wait_ge(g_step, j * 8 + 9)
                    if valid(j - 1, 0, NCH):
                        dve.wait_ge(hlt_ready, j)
                    dve.scalar_tensor_tensor(hl[:, 0:R3], bank[4][:, 0:R3], IWS, keep, ALU.mult, ALU.mult
                                             ).then_inc(hl_done, 1)
                j, v = i + 1, (u + 1) % 4
                if valid(j, 0, NCH):
                    dve.wait_ge(ct3_hi, j + 1)
                    dve.scalar_tensor_tensor(c3t[v % 2][1], bank[1][:, :], IWS, c3t[v % 2][0], ALU.mult, ALU.subtract
                                             ).then_inc(ct3_split, 1)
                j, v = i, u
                if valid(j, 0, NCH):
                    dve.wait_ge(hlt_ready, j + 1)
                    dve.tensor_copy(hlt[0], bank[5][:, 0:P]).then_inc(hlt_hi, 1)
                    dve.wait_ge(hlt_hi, j + 1)
                    dve.tensor_tensor(hlt[1], bank[5][:, 0:P], hlt[0], ALU.subtract).then_inc(hlt_split, 1)
                j, v = i + 2, (u + 2) % 4
                if valid(j, 0, NCH):
                    dve.wait_ge(xt3_hi, j + 1)
                    dve.tensor_tensor(x3t[v % 2][1], bank[0][:, :], x3t[v % 2][0], ALU.subtract).then_inc(xt3_split, 1)
                if valid(i + 2, 2, NCH):
                    copy_w3(i + 2, (u + 2) % 2)
                j, v = i, u
                if valid(j, 0, NCH):
                    dve.wait_ge(fin_ready, j + 1)
                    dve.wait_ge(x3b_done, j + 1)
                    if valid(j - 2, 0, NCH):
                        dve.wait_ge(fin_stored[v % 2], slot_count(j - 2, v, 2))
                    dve.scalar_tensor_tensor(fin[v % 2], bank[3][:, :], IWS, x3b[v], ALU.mult, ALU.add
                                             ).then_inc(fin_done, 1)

            run_c(dve, step_c)

        @block.tensor
        def _(pe):
            pe.sem_inc(down_ready, CR_DOWN)
            pe.wait_ge(const_in, 64)
            pe.wait_ge(table_step, 10)
            pe.matmul(bank[7][:, 0:B], b_sess, onehot, start=True, stop=True).then_inc(table_mm, 1)
            pe.wait_ge(table_step, 20)
            pe.matmul(bank[6][:, 0:NCH * GB], later, spread, start=True, stop=False)
            pe.matmul(bank[6][:, 0:NCH * GB], same, const("ones"), start=False, stop=True).then_inc(table_mm, 1)
            pe.wait_ge(table_step, 22)
            pe.matmul(bank[7][:, 0:NCH * GB], const("number"), at_batch, start=True, stop=True)
            pe.matmul(bank[7][:, NCH * GB:2 * NCH * GB], own_adapter, at_batch, start=True, stop=True
                      ).then_inc(table_mm, 1)
            with pe.Fori(0, NA // 2) as it:
                for p in range(2):
                    i = it * 2 + p
                    lav = la[p].rearrange("p (h c m) -> p h c m", h=2, m=P)
                    xv = [xt[p][h].rearrange("p (k t) -> p k t", k=KH) for h in range(2)]
                    pe.wait_ge(lora_split, i * PIECES + 2)
                    pe.wait_ge(x_split, i + 2)
                    for kind in range(2):
                        for k in range(KH):
                            c = kind * KH + k
                            last = mm3(pe, bank[4 + kind][:, 0:TA],
                                       [lav[:, h, c, :] for h in range(2)],
                                       [xv[h][:, k, :] for h in range(2)], k == 0, k == KH - 1)
                        last.then_inc(t_ready, 1)
                    for f in range(NF):
                        q = (p + f) % 2
                        pe.wait_ge(prep_lo, f + 1)
                        pe.wait_ge(prod_done, i * NF + f + 1)
                        for g in range(2):
                            o = bank[2 * g + q][:, 0:TA]
                            for k in range(KH):
                                mm3(pe, o, [wgu[h][:, f, g, k, :] for h in range(2)],
                                    [xv[h][:, k, :] for h in range(2)], k == 0, False)
                            if f == 0:
                                pe.wait_ge(t_split, i * 3 + g + 1)
                                pe.wait_ge(lora_split, i * PIECES + 3)
                            if f == 2:
                                pe.wait_ge(lora_split, i * PIECES + 4)
                            at = (g * NF + f) * P
                            mm3(pe, o, [lb[p][:, h * LB + at:h * LB + at + P] for h in range(2)],
                                t_part[g], False, True).then_inc([gate_ready, up_ready][g], 1)
                    for f in range(NF):
                        pe.wait_ge(act_split, i * NF + f + 1)
                        last = mm3(pe, bank[4][:, 0:TA], [lav[:, h, 2 * KH + f, :] for h in range(2)],
                                   [act[h][:, f, :] for h in range(2)], f == 0, f == NF - 1)
                    last.then_inc(t_ready, 1)
                    pe.wait_ge(prep_lo, len(jobs))
                    for hc in range(KH):
                        o = bank[6 + hc % 2][:, 0:TA]
                        pe.wait_ge(c0_split, i * 4 + hc + 1)
                        for f in range(NF):
                            mm3(pe, o, [wdn[h][:, f, hc * P:(hc + 1) * P] for h in range(2)],
                                [act[h][:, f, :] for h in range(2)], f == 0, False)
                        if hc == 0:
                            pe.wait_ge(t_split, i * 3 + 3)
                        at = 2 * FP + hc * P
                        mm3(pe, o, [lb[p][:, h * LB + at:h * LB + at + P] for h in range(2)],
                            t_part[2], False, True).then_inc(down_ready, 1)
            pe.wait_ge(c0_split, 4 * NA + CR_C0)
            with pe.Fori(0, NB // 2) as it:
                for p in range(2):
                    i = it * 2 + p
                    pe.wait_ge(ct_loaded[p], (it + 1) * 32)
                    for f in range(NF):
                        q = (p + f) % 2
                        pe.wait_ge(wq_loaded[f], 32)
                        pe.wait_ge(prod2_done, i * NF + f + 1)
                        for g in range(2):
                            o = bank[2 * g + q][:, :]
                            for k in range(KH):
                                last = mm3(pe, o, [wgu[h][:, f, g, k, :] for h in range(2)],
                                           [ct[p][h][:, k, :] for h in range(2)], k == 0, k == KH - 1)
                            last.then_inc([gate2_ready, up2_ready][g], 1)
                    pe.wait_ge(wq_loaded[NF], 32)
                    for g in range(4):
                        pe.wait_ge(out16_done, i * 4 + 4)
                        for f in range(NF):
                            if g == 0:
                                pe.wait_ge(act2_split, i * NF + f + 1)
                            last = mm3(pe, bank[4 + g][:, :], [act2[h][:, f, g * P:(g + 1) * P] for h in range(2)],
                                       [wdn[h][:, f, :] for h in range(2)], f == 0, f == NF - 1)
                        last.then_inc(down2_ready, 1)
            pe.wait_ge(out16_done, 4 * NB + 4)
            pe.wait_ge(prod2_done, NF * NB + CR_PROD)
            pe.wait_ge(wb_loaded, 32)
            pe.wait_ge(deq2_done, NB + 1)

            def step_b(i, u):
                g, v = i, u
                cv = [w.rearrange("p (k t) -> p k t", k=KH) for w in c1[v % 2]]
                if valid(g, 0, NG):
                    pe.wait_ge(c1_split, g + 1)
                    if valid(g - 1, 0, NG):
                        pe.wait_ge(hw_done, g)
                    for k in range(KH):
                        last = mm3(pe, bank[4][:, 0:WAR], [w[:, k, :] for w in cv], [w[:, k, :] for w in w_ar1],
                                   k == 0, k == KH - 1)
                    last.then_inc(router_ready, 1)
                g, v = i - 1, (u - 1) % 4
                if valid(g, 0, NG):
                    pe.wait_ge(x2_split, g + 1)
                    pe.wait_ge(bd2_ready, g + 1)
                    if valid(g - 1, 0, NG):
                        pe.wait_ge(c2_split, g)
                    for k in range(KH):
                        last = mm3(pe, bank[6][:, k * P:(k + 1) * P], [w[:, k * P:(k + 1) * P] for w in x2_part[v % 2]],
                                   bd2[v % 2], True, True)
                    last.then_inc(c2_ready, 1)
                g, v = i, u
                if valid(g, 0, NG):
                    if valid(g - 1, 0, NG):
                        pe.wait_ge(x2_done, g)
                    for k in range(KH):
                        mm3(pe, bank[3][:, :], [w[:, k, :] for w in cv], [w[:, k, :] for w in w_base1], k == 0, False)
                g, v = i + 1, (u + 1) % 4
                if valid(g, 0, NG):
                    pe.wait_ge(hid_split, 2 * g + 2)
                    if valid(g - 1, 0, NG):
                        pe.wait_ge(c1_step, 3 * g - 2)
                    for k in range(KH):
                        for pair in range(2):
                            at = k * P + pair * 2 * S
                            last = mm3(pe, bank[2][:, at:at + 2 * S],
                                       [w[:, k * P:(k + 1) * P] for w in hid[v % 2][pair]],
                                       [w[:, 0, :] for w in w_mix1], True, True)
                    last.then_inc(mixed_ready, 1)
                g, v = i, u
                if valid(g, 0, NG):
                    pe.wait_ge(hw_done, g + 1)
                    if valid(g - 1, 0, NG):
                        pe.wait_ge(hwt_split, g)
                    pe.transpose(bank[5][:, 0:P], hw, const("ident")).then_inc(hwt_ready, 1)
                g, v = i + 2, (u + 2) % 4
                if valid(g, 0, NG):
                    pe.wait_ge(x1_split, g + 1)
                    pe.wait_ge(bd1_ready, g + 1)
                    if valid(g - 1, 0, NG):
                        pe.wait_ge(gelu_done, 2 * g)
                    for pair in range(2):
                        mm3(pe, bank[pair][:, :], [w[:, pair * P:(pair + 1) * P] for w in bd1[v % 2]],
                            x1_part[v % 2], True, True).then_inc(hid_ready, 1)
                g, v = i, u
                if valid(g, 0, NG):
                    pe.wait_ge(hwt_split, g + 1)
                    mm3(pe, bank[3][:, :], hwt, [w[:, 0, :] for w in w_b1], False, True).then_inc(x2_ready, 1)
                g, v = i - 1, (u - 1) % 4
                if valid(g, 0, NG):
                    pe.wait_ge(c2_split, g + 1)
                    if valid(g - 1, 0, NG):
                        pe.wait_ge(x3_done, g)
                    for k in range(KH):
                        last = mm3(pe, bank[7][:, :], [w[:, k * P:(k + 1) * P] for w in c2[v % 2]],
                                   [w[:, k, :] for w in w_2], k == 0, k == KH - 1)
                    last.then_inc(y3_ready, 1)

            run_b(pe, step_b)
            pe.wait_ge(wc_loaded, 32)
            pe.wait_ge(x3_done, NG)

            def step_c(i, u):
                j, v = i, u
                if valid(j, 0, NCH):
                    pe.wait_ge(ct3_split, j + 1)
                    if valid(j - 1, 0, NCH):
                        pe.wait_ge(hl_done, j)
                    for k in range(KH):
                        last = mm3(pe, bank[4][:, 0:WAG], [w[:, k * P:(k + 1) * P] for w in c3t[v % 2]],
                                   [w[:, k, :] for w in w_ag3], k == 0, k == KH - 1)
                    last.then_inc(ag3_ready, 1)
                j, v = i + 1, (u + 1) % 4
                if valid(j, 0, NCH):
                    pe.wait_ge(xt3_split, j + 1)
                    if valid(j - 1, 0, NCH):
                        pe.wait_ge(ct3_split, j)
                    pe.wait_ge(w3_copied, 2 * (j + 1))
                    for hc in range(KH):
                        for k in range(KH):
                            last = mm3(pe, bank[1][:, hc * P:(hc + 1) * P],
                                       [w[:, k * H + hc * P:k * H + (hc + 1) * P] for w in w3_now[v % 2]],
                                       [w[:, k * P:(k + 1) * P] for w in x3t[v % 2]], k == 0, k == KH - 1)
                    last.then_inc(cond3_ready, 1)
                j, v = i + 2, (u + 2) % 4
                if valid(j, 0, NCH):
                    pe.wait_ge(x3_loaded[v], slot_count(j, v, 4))
                    if valid(j - 1, 0, NCH):
                        pe.wait_ge(xt3_split, j)
                    for k in range(KH):
                        last = pe.transpose(bank[0][:, k * P:(k + 1) * P], x3_in[v][:, k * P:(k + 1) * P],
                                            const("ident"))
                    last.then_inc(xt3_ready, 1)
                j, v = i, u
                if valid(j, 0, NCH):
                    pe.wait_ge(hl_done, j + 1)
                    if valid(j - 1, 0, NCH):
                        pe.wait_ge(hlt_split, j)
                    pe.transpose(bank[5][:, 0:P], hl, const("ident")).then_inc(hlt_ready, 1)
                    if valid(j - 1, 0, NCH):
                        pe.wait_ge(fin_done, j)
                    for k in range(KH):
                        last = mm3(pe, bank[3][:, :], [w[:, k * P:(k + 1) * P] for w in c3t[v % 2]],
                                   [w[:, k, :] for w in w_base3], k == 0, False)
                    last.then_inc(ag3_ready, 1)
                    pe.wait_ge(hlt_split, j + 1)
                    mm3(pe, bank[3][:, :], hlt, [w[:, 0, :] for w in w_b3], False, True).then_inc(fin_ready, 1)

            run_c(pe, step_c)


def block_layout(gate, up, down, fill):
    gu = np.full((2, H, FP), fill, gate.dtype)
    gu[0, :, :FF], gu[1, :, :FF] = gate, up
    dn = np.full((FP, H), fill, down.dtype)
    dn[:FF] = down
    gu = gu.reshape(2, KH, P, NF, P).transpose(2, 3, 0, 1, 4).reshape(P, GU)
    dn = dn.reshape(NF, P, H).transpose(1, 0, 2).reshape(P, DN)
    return np.ascontiguousarray(np.concatenate([gu, dn], axis=1))


def row_layout(gate, up, down):
    n = FP * gate.shape[1] // FF
    gu = np.zeros((2, KH, n), gate.dtype)
    gu[0, :, :gate.shape[1]], gu[1, :, :up.shape[1]] = gate, up
    gu = gu.reshape(2, KH, NF, n // NF).transpose(2, 0, 1, 3).reshape(-1)
    return np.ascontiguousarray(np.concatenate([gu, down.reshape(-1)]).reshape(1, -1))


def arrays(i):
    i = {k: np.asarray(v) for k, v in i.items()}
    d = {}
    x = i["x"].reshape(TOK, H)
    d["x"] = x
    d["xt"] = np.ascontiguousarray(x.T)
    d["w_cond"] = block_layout(i["L0_cond_W_gate"].T, i["L0_cond_W_up"].T, i["L0_cond_W_down"].T, 0)
    a = [i[f"L0_cond_A_{n}"][0] for n in ("gate", "up")]
    ad = np.zeros((ADAPT, RANK, FP), np.float32)
    ad[:, :, :FF] = i["L0_cond_A_down"][0]
    parts = [v.reshape(ADAPT, RANK, -1, P).transpose(0, 3, 2, 1).reshape(ADAPT * P, -1) for v in (*a, ad)]
    d["lora_a"] = np.ascontiguousarray(np.concatenate(parts, axis=1))
    bs = []
    for n in ("gate", "up"):
        b = np.zeros((ADAPT, RANK, FP), np.float32)
        b[:, :, :FF] = i[f"L0_cond_B_{n}"][0].transpose(0, 2, 1)
        bs.append(b.reshape(ADAPT * RANK, FP))
    bs.append(i["L0_cond_B_down"][0].transpose(0, 2, 1).reshape(ADAPT * RANK, H))
    d["lora_b"] = np.ascontiguousarray(np.concatenate(bs, axis=1))
    d["q"] = block_layout(*(np.repeat(i[f"L0_ffn_{n}_qweight"], 8, axis=0) for n in ("gate", "up", "down")), 0)
    d["z"] = row_layout(*(i[f"L0_ffn_{n}_zeros"] for n in ("gate", "up", "down")))
    d["s"] = row_layout(*(i[f"L0_ffn_{n}_scales"] for n in ("gate", "up", "down")))
    p = np.arange(P)
    b = np.arange(B)
    level = np.searchsorted([8, 16, 32], np.arange(R3), side="right")
    d["consts"] = np.concatenate([np.broadcast_to(v, (P, CONSTS[n][1])) for n, v in {
        "col": p[:, None], "mod16": p[:, None] % RANK, "mod32": p[:, None] % S,
        "hcol": p[:, None] + P * np.arange(KH), "iota8": np.arange(8), "sign": [1, -1], "one": [1, 1],
        "level": level, "blocks": p[:, None] // S == np.arange(GB), "number": p[:, None] + 1, "before": p[:, None] < b,
        "places": np.arange(NCH * GB), "ones": np.ones(NCH * GB), "ident": np.eye(P),
        "own_batch": p[:, None] // RANK == np.arange(TA) // S}.items()], axis=1).astype(np.float32)
    d["shift"] = np.concatenate([(p % 8 * 4)[:, None], np.repeat((p % 2 * 4)[:, None], 7, axis=1)], axis=1).astype(np.int32)
    a0, sess, seq, cond, a3, lens = (i[n] for n in (
        "itok_B_2_6", "itok_B_0_7", "itok_B_2182_4065", "itok_B_0_15", "itok_B_3_7", "_lenS"))

    def own(v, rows):
        return np.repeat(v.reshape(-1, P // rows), rows, axis=1).T

    d["ids"] = np.ascontiguousarray(np.concatenate([np.broadcast_to(v, (P, IDS[n][1])) for n, v in {
        "lora0": a0, "lora0_own": own(a0, RANK), "sess_own": own(sess, S), "cond_own": own(cond, S),
        "len_own": own(lens, S), "sess": sess, "seq": seq, "adapter": a3, "adapter_own": a3[:, None]}.items()], axis=1))
    d["biases"] = np.ascontiguousarray(np.broadcast_to(np.concatenate(
        [i[n] for n in ("L1_cond_b2", "L1_ffn_b_base", "L2_ffn_bias", "L3_ffn_b", "L3_ffn_gate_b")]), (P, NBIAS)))
    bs = np.zeros((P, P), np.float32)
    bs[:NSESS, :HID] = bs[:NSESS, HID:] = i["L1_cond_b_sess"]
    d["b_sess"] = bs
    d["w_sess"] = i["L1_cond_W_sess"].reshape(NSESS * S, HID)
    d["w_mix2"] = i["L2_cond_weights"].reshape(NCOND * S, S)

    def k_tiles(w):
        return w.reshape(KH, P, -1).transpose(1, 0, 2).reshape(P, -1)

    mix = np.zeros((2, HID, 2, S), np.float32)
    mix[0, :, 0], mix[1, :, 1] = i["L1_cond_W2"], i["L1_cond_W2"]
    b3 = np.zeros((P, H), np.float32)
    b3[:R3] = i["L3_ffn_B"].T
    d["late"] = np.ascontiguousarray(np.concatenate([
        k_tiles(i["L1_ffn_W_base"].T),
        k_tiles(np.concatenate([i["L1_ffn_A"].reshape(EXP * R1, H), i["L1_ffn_W_router"]]).T),
        i["L1_ffn_B"].transpose(0, 2, 1).reshape(P, H), mix.reshape(P, 2 * S),
        k_tiles(i["L3_ffn_W"].T), k_tiles(np.concatenate([i["L3_ffn_A"], i["L3_ffn_gate_w"]]).T), b3,
        *(k_tiles(w.T) for w in i["L3_cond_weight"])], axis=1))
    d["p2"] = np.ascontiguousarray(k_tiles(np.repeat(i["L2_ffn_weight_packed"].reshape(H, H // 2).T, 2, axis=0)))
    d["s2"] = np.ascontiguousarray(k_tiles(np.repeat(i["L2_ffn_weight_scale"].reshape(H, H // 32).T, 32, axis=0)))
    d["m2"] = np.ascontiguousarray(k_tiles(np.repeat(
        i["L2_ffn_weight_var_mask"].reshape(H, H // 32).T, 32, axis=0)))
    return d


def kernel(**inputs):
    import concourse.bacc as bacc
    from concourse.bass_utils import run_bass_kernel_spmd

    nc = bacc.Bacc("TRN2", target_bir_lowering=False, num_devices=1)
    ins = arrays(inputs)
    d = {n: nc.dram_tensor(n + "_in", a.shape, mybir.dt.from_np(a.dtype), kind="ExternalInput").ap()
         for n, a in ins.items()}
    out = nc.dram_tensor("out", (TOK, H), F32, kind="ExternalOutput").ap()
    program(nc, d, out)
    got = run_bass_kernel_spmd(nc, [{n + "_in": a for n, a in ins.items()}], core_ids=[0])
    return got.results[0]["out"].reshape(B, S, H)
```
